# Optimizing a Trainium2 kernel written in Bass

```python
import numpy as np
import jax
import jax.numpy as jnp

def _softmax(x, axis=-1):
    return jax.nn.softmax(x, axis=axis)
def _gelu(x):
    return jax.nn.gelu(x, approximate=True)
def _silu(x):
    return jax.nn.silu(x)
def _sigmoid(x):
    return jax.nn.sigmoid(x)
def _layernorm(x, axis=-1, eps=1e-5):
    m = jnp.mean(x, axis=axis, keepdims=True)
    v = jnp.var(x, axis=axis, keepdims=True)
    return (x - m) / jnp.sqrt(v + eps)
def _scatter_add(tgt, idx, src, axis=0):
    return tgt.at[idx].add(src)
def _segment_sum(src, seg, n):
    return jax.ops.segment_sum(src, seg, n)

kernel_name = 'mk_conv_preact_d2_conv_nhwc32_b144b7'

def setup_inputs(seed: int = 0):
    np.random.seed(seed)
    _w = jnp.asarray
    def _rec_inputs():
        import jax
        import jax.numpy as jnp
        _gk = jax.random.key(seed)
        x = -7.109e-05 + 0.9999 * jax.random.normal(jax.random.fold_in(_gk, 1), (8, 512, 512, 32), jnp.float32)
        return x
    x = _rec_inputs()
    def _L0_conv_setup():
        import jax, jax.numpy as jnp
        import numpy as np
        B, H, Wd, C = (8, 512, 512, 32)
        MODES = 32
        key = jax.random.key(seed)
        k1, k2 = jax.random.split(key)
        x = jax.random.normal(k1, (B, H, Wd, C), dtype=jnp.float32)
        scale = (2.0 / (C + C)) ** 0.5
        W = jax.random.normal(k2, (MODES, MODES, C, C), dtype=jnp.float32) * scale
        return {'x': x, 'W': W}
    _L0_conv_all = _L0_conv_setup()
    _L0_conv_in = {k: v for k, v in _L0_conv_all.items() if k in ('W', )}
    del _L0_conv_all

    def _L1_conv_setup():
        import jax, jax.numpy as jnp
        import numpy as np
        from jax import lax
        EPSILON = 1e-06

        def _sobel_kernels(channels, dtype):
            kx = np.array([[1, 0, -1], [2, 0, -2], [1, 0, -1]], np.float32) / 4.0
            ky = np.array([[1, 2, 1], [0, 0, 0], [-1, -2, -1]], np.float32) / 4.0
            kx = jnp.asarray(np.tile(kx[:, :, None, None], [1, 1, 1, channels]), dtype)
            ky = jnp.asarray(np.tile(ky[:, :, None, None], [1, 1, 1, channels]), dtype)
            return (kx, ky)

        def _avg_pool3_same(x):
            dims, strides = ((1, 3, 3, 1), (1, 1, 1, 1))
            sums = lax.reduce_window(x, jnp.array(0, x.dtype), lax.add, dims, strides, 'SAME')
            ones = jnp.ones((1, x.shape[1], x.shape[2], 1), x.dtype)
            counts = lax.reduce_window(ones, jnp.array(0, x.dtype), lax.add, dims, strides, 'SAME')
            return sums / counts

        def _depthwise3(x, kernel):
            c = x.shape[-1]
            return lax.conv_general_dilated(x, kernel, window_strides=(1, 1), padding='SAME', dimension_numbers=('NHWC', 'HWIO', 'NHWC'), feature_group_count=c)
        key = jax.random.key(seed)
        x = jax.random.normal(key, (8, 512, 512, 32), dtype=jnp.float32)
        return {'x': x}
    _L1_conv_all = _L1_conv_setup()
    _L1_conv_in = {k: v for k, v in _L1_conv_all.items() if k in ()}
    del _L1_conv_all

    return {
        "x": x,
        "L0_conv_W": _L0_conv_in["W"],
    }

def reference(x, L0_conv_W):
    import jax
    import jax.numpy as jnp
    def _L0_conv_ref(x, W):
        import jax, jax.numpy as jnp
        import numpy as np
        B, H, Wd, C = (8, 512, 512, 32)
        MODES = 32
        modes = W.shape[0]
        h, w = (x.shape[1], x.shape[2])
        xf = jnp.fft.rfft2(x, axes=(1, 2))
        low = xf[:, :modes, :modes, :]
        out_low = jnp.einsum('bxyc,xycd->bxyd', low, W.astype(xf.dtype))
        out_f = jnp.pad(out_low, ((0, 0), (0, xf.shape[1] - modes), (0, xf.shape[2] - modes), (0, 0)))
        return jnp.fft.irfft2(out_f, s=(h, w), axes=(1, 2))

    def _L1_conv_ref(x):
        import jax, jax.numpy as jnp
        import numpy as np
        from jax import lax
        EPSILON = 1e-06

        def _sobel_kernels(channels, dtype):
            kx = np.array([[1, 0, -1], [2, 0, -2], [1, 0, -1]], np.float32) / 4.0
            ky = np.array([[1, 2, 1], [0, 0, 0], [-1, -2, -1]], np.float32) / 4.0
            kx = jnp.asarray(np.tile(kx[:, :, None, None], [1, 1, 1, channels]), dtype)
            ky = jnp.asarray(np.tile(ky[:, :, None, None], [1, 1, 1, channels]), dtype)
            return (kx, ky)

        def _avg_pool3_same(x):
            dims, strides = ((1, 3, 3, 1), (1, 1, 1, 1))
            sums = lax.reduce_window(x, jnp.array(0, x.dtype), lax.add, dims, strides, 'SAME')
            ones = jnp.ones((1, x.shape[1], x.shape[2], 1), x.dtype)
            counts = lax.reduce_window(ones, jnp.array(0, x.dtype), lax.add, dims, strides, 'SAME')
            return sums / counts

        def _depthwise3(x, kernel):
            c = x.shape[-1]
            return lax.conv_general_dilated(x, kernel, window_strides=(1, 1), padding='SAME', dimension_numbers=('NHWC', 'HWIO', 'NHWC'), feature_group_count=c)
        kx, ky = _sobel_kernels(x.shape[-1], x.dtype)
        pooled = _avg_pool3_same(x)
        grad_x = _depthwise3(pooled, kx)
        grad_y = _depthwise3(pooled, ky)
        return jnp.sqrt(grad_x * grad_x + grad_y * grad_y + EPSILON)

    def _gn(v, G=16, eps=1e-5):
        B_, H_, W_, C_ = v.shape
        g = v.reshape(B_, H_, W_, G, C_ // G)
        m = jnp.mean(g, axis=(1, 2, 4), keepdims=True)
        s = jnp.var(g, axis=(1, 2, 4), keepdims=True)
        return ((g - m) / jnp.sqrt(s + eps)).reshape(v.shape)

    def _ln_c(v, eps=1e-6):
        m = jnp.mean(v, axis=-1, keepdims=True)
        s = jnp.var(v, axis=-1, keepdims=True)
        return (v - m) / jnp.sqrt(s + eps)

    def _ln_t(v, eps=1e-5):
        m = jnp.mean(v, axis=-1, keepdims=True)
        s = jnp.var(v, axis=-1, keepdims=True)
        return (v - m) / jnp.sqrt(s + eps)

    def _to_tokens(v):
        B_, H_, W_, C_ = v.shape
        return v.reshape(B_, H_ * W_, C_)
    def _from_tokens(t, like):
        return t.reshape(like.shape)

    x = x + _L0_conv_ref(_gn(x), L0_conv_W)
    x = x + _L1_conv_ref(_gn(x))
    return x


_drawn_inputs = setup_inputs


def setup_inputs(seed=0):
    import zlib

    import numpy as np

    out = dict(_drawn_inputs(seed))
    spreads = {}
    factors = {}
    for name, (base, spread) in spreads.items():
        noise = np.random.default_rng([zlib.crc32(name.encode()), seed]).standard_normal(out[name].shape)
        drawn = base * np.exp(spread * noise) if base else spread * noise
        out[name] = jnp.asarray(drawn.astype(out[name].dtype))
    for name, factor in factors.items():
        out[name] = (out[name] * factor).astype(out[name].dtype)
    return out
```

```python
from contextlib import ExitStack

import numpy as np

import concourse.bass as bass
from concourse import mybir

F32 = mybir.dt.float32
F32R = mybir.dt.float32r
ALU = mybir.AluOpType
ACT = mybir.ActivationFunctionType
AX = mybir.AxisListType

B, H, W, C = 8, 512, 512, 32
N = 512
MODES = 32
GROUP = 2
GROUPS = C // GROUP
BG = B * GROUPS
P = 128
RI = 2 * MODES
EPS_GN = 1e-5
EPS_GRAD = 1e-6

HALF = W // 2
WIN = HALF + 2
WB = WIN + 2
PAIRS = WB - 1
ROW0 = [0, 124, 248, 372, 480]
ROWS = [128, 128, 128, 128, 32]
OUT = [(0, 126), (126, 250), (250, 374), (374, 498), (498, 512)]
VARIANT = [0, 1, 1, 1, 2]
BLOCKS = len(ROW0)
TURNS = 2 * B
STEPS = BLOCKS * GROUPS
RING = 8

CW = 32
CHUNKS = W // CW
HB = H // P
XRING = 4
WBLK = W // P
PER_BLK = P // CW
SUB = 512 // C


def tables():
    k = np.arange(MODES)
    ang = 2 * np.pi * np.outer(np.arange(N), k) / N
    cos, sin = np.cos(ang), np.sin(ang)
    fh = np.concatenate([cos, -sin], 1).reshape(HB, P, RI).transpose(1, 0, 2)
    fw = np.stack([np.concatenate([cos, -sin], 1), np.concatenate([sin, cos], 1)], 1)
    fw = fw.reshape(WBLK, P, 2, RI).transpose(1, 0, 2, 3)
    alpha = np.where(k == 0, 1.0, 2.0)
    rows = np.concatenate([cos * alpha, sin * alpha], 1).T / N
    left = np.concatenate([-(1.5 * rows[:, :1] + 0.5 * rows[:, 1:2]), 0.5 * (rows[:, :1] + rows[:, 1:2]),
                           rows[:, :WIN]], 1)
    right = np.concatenate([rows[:, W - WIN:], 0.5 * (rows[:, -1:] + rows[:, -2:-1]),
                            -(1.5 * rows[:, -1:] + 0.5 * rows[:, -2:-1])], 1)
    ew = np.stack([left, right], 1)
    eh = np.zeros((P, BLOCKS, P))
    both = np.concatenate([cos, -sin], 1).T / N
    for b, (r0, n) in enumerate(zip(ROW0, ROWS)):
        eh[:, b, :n] = np.tile(both[:, r0:r0 + n], (2, 1))
    pool = sum(np.eye(H, k=d) for d in (-1, 0, 1))
    pool[0] *= 1.5
    pool[-1] *= 1.5
    smooth = (2 * np.eye(H) + np.eye(H, k=1) + np.eye(H, k=-1)) @ pool
    diff = (np.eye(H, k=-1) - np.eye(H, k=1)) @ pool
    hm = np.zeros((P, 3, 2, P))
    for b in (0, 1, 4):
        r0, n = ROW0[b], ROWS[b]
        for i, m in enumerate((smooth, diff)):
            hm[:n, VARIANT[b], i, :n] = m[r0:r0 + n, r0:r0 + n].T
    sign = np.concatenate([alpha, -alpha])
    beta = np.where(k == 0, 0.5, 2.0)
    ws = np.stack([2 * sign, np.concatenate([beta, beta])], 1) / N**2 / (GROUP * H * W)
    ws = np.repeat(ws[:, :, None], P, 2)
    t = {"fh": fh, "fw": fw, "ew": ew, "eh": eh, "hm": hm, "ws": ws, "ones": np.full((P, P), 1 / P),
         "onerow": np.full((1, P), 1 / (GROUP * N**2)), "ident": np.eye(P)}
    return {n: np.ascontiguousarray(a, np.float32) for n, a in t.items()}


def spectral_gradient_kernel(nc, x, w_modes, tab, out, od):
    ctx = ExitStack()
    with ctx:
        def sb(name, shape, dt=F32, at=ctx):
            return at.enter_context(nc.sbuf_tensor(name, shape, dt))

        def ps(name, shape, at):
            return at.enter_context(nc.psum_tensor(name, shape, F32))

        def sem(name):
            return ctx.enter_context(nc.semaphore(name))

        ew_t = sb("ew_t", [RI, 2, WB])
        eh_hi = sb("eh_hi", [P, BLOCKS, P], F32R)
        eh_lo = sb("eh_lo", [P, BLOCKS, P], F32R)
        hmat = sb("hmat", [P, 3, 4, P], F32R)
        mean1 = sb("mean1", [P, BG])
        gscale = sb("gscale", [P, BG])
        eps_t = sb("eps_t", [P, 1])

        spectra = ExitStack()
        with spectra:
            fh_t = sb("fh_t", [P, HB, RI], at=spectra)
            fw_t = sb("fw_t", [P, WBLK, 2, RI], at=spectra)
            ident = sb("ident_t", [P, P], at=spectra)
            ones = sb("ones_t", [P, P], at=spectra)
            onerow = sb("onerow_t", [1, P], at=spectra)
            ws_t = sb("ws_t", [RI, 2, P], at=spectra)
            wt = sb("wt", [P, MODES // 4, MODES, C], at=spectra)
            xs = sb("xs", [RI, B, C, MODES], at=spectra)
            ag = sb("ag", [P, B, GROUPS, 2], at=spectra)
            forward_pass(nc, sb, ps, sem, x, w_modes, tab, fh_t, fw_t, ident, ones, onerow, ws_t, wt, xs, ag,
                         ew_t, eh_hi, eh_lo, hmat, eps_t)
            modes_pass(nc, sb, ps, sem, od, ident, ones, onerow, ws_t, wt, xs, ag, mean1, gscale)
        gradient_pass(nc, sb, ps, sem, x, out, od, ew_t, eh_hi, eh_lo, hmat, mean1, gscale, eps_t)


def need(engine, semaphore, count):
    if not (isinstance(count, int) and count <= 0):
        engine.wait_ge(semaphore, count)


def alone(engine, passed):
    engine.sem_inc(passed, 1)


def rolled(engine, count, body):
    body(0)
    with engine.Fori(1, count) as i:
        body(i)


def forward_pass(nc, sb, ps, sem, x, w_modes, tab, fh_t, fw_t, ident, ones, onerow, ws_t, wt, xs, ag,
                 ew_t, eh_hi, eh_lo, hmat, eps_t):
    with ExitStack() as fwd:
        xa = sb("xa", [P, XRING, HB, CW * C], at=fwd)
        zs = sb("zs", [RI, 2, P, C], at=fwd)
        zt = sb("zt", [P, C, RI], at=fwd)
        bn = sb("bn", [P, GROUPS, CHUNKS, 6], at=fwd)
        merged = sb("merged", [P, GROUPS, 2], at=fwd)
        eh_raw = sb("eh_raw", [P, BLOCKS, P], at=fwd)
        hm_raw = sb("hm_raw", [P, 3, 2, P], at=fwd)
        zps = [ps(f"zps{i}", [RI, 512], fwd) for i in range(2)]
        tps = [ps(f"tps{i}", [P, 512], fwd) for i in range(2)]
        xps = ps("xps", [RI, C * MODES], fwd)

        loaded = [sem(f"chunk_loaded{i}") for i in range(XRING)]
        tables_in, weights_in = sem("tables_in"), sem("weights_in")
        chunk_counted = sem("chunk_counted")
        z_done, z_used = sem("z_done"), sem("z_used")
        t_done, t_used = sem("t_done"), sem("t_used")
        modes_done, modes_used = sem("modes_done"), sem("modes_used")
        split_hi, split_lo = sem("split_hi"), sem("split_lo")
        image_merged, passed = sem("image_merged"), sem("forward_passed")

        loads = [(fh_t, "fh"), (fw_t, "fw"), (ident, "ident"), (ones, "ones"), (onerow, "onerow"), (ws_t, "ws"),
                 (ew_t, "ew"), (eh_raw, "eh"), (hm_raw, "hm")]
        x_v = x.rearrange("b (t p) w c -> b p t (w c)", p=P)
        w_v = w_modes.rearrange("(r s) q c d -> r c s q d", r=4)
        CH = 512 // RI
        ZB = CW // SUB

        with nc.Block() as block:
            @block.sync
            def _(sp):
                for t, name in loads:
                    sp.dma_start(t[:], tab[name]).then_inc(tables_in, 16)

                def ring(i):
                    for j in range(XRING):
                        need(sp, z_done, ((i - 1) * XRING + j + 1) * ZB)
                        need(sp, chunk_counted, (i - 1) * XRING + j + 1)
                        at = (i * XRING + j) % CHUNKS * (CW * C)
                        sp.dma_start(xa[:, j], x_v[i * XRING // CHUNKS, :, :, bass.ds(at, CW * C)]
                                     ).then_inc(loaded[j], 16)

                rolled(sp, B * CHUNKS // XRING, ring)

            @block.gpsimd
            def _(pool):
                nc.gpsimd.memset(eps_t[:], EPS_GRAD)
                for r in range(4):
                    for s in range(MODES // 4):
                        pool.dma_start(wt[r * C:(r + 1) * C, s], w_v[r, :, s]).then_inc(weights_in, 16)
                pool.wait_ge(weights_in, 16 * MODES)

            @block.tensor
            def _(pe):
                pe.wait_ge(tables_in, 16 * len(loads))

                def image(b):
                    for k in range(WBLK):
                        blk = b * WBLK + k
                        for j in range(PER_BLK):
                            chunk = blk * PER_BLK + j
                            pe.wait_ge(loaded[j], 16 * (blk + 1))
                            for s in range(ZB):
                                need(pe, z_used, (chunk - 1) * ZB + s + 1)
                                for t in range(HB):
                                    last = nc.tensor.matmul(
                                        zps[s][:], fh_t[:, t], xa[:, j, t, s * 512:(s + 1) * 512],
                                        start=(t == 0), stop=(t == HB - 1))
                                last.then_inc(z_done, 1)
                        pe.wait_ge(z_used, (blk + 1) * PER_BLK * ZB)
                        for o in range(C // CH):
                            need(pe, t_used, blk * (C // CH) + o - 1)
                            alone(pe, passed)
                            for c in range(CH):
                                last = nc.tensor.transpose(tps[o % 2][:, c * RI:(c + 1) * RI],
                                                           zs[:, k % 2, :, o * CH + c], ident[0:RI, 0:RI])
                            last.then_inc(t_done, 1)
                        if k == 0:
                            need(pe, modes_used, b)
                        for half in range(2):
                            pe.wait_ge(t_used, blk * (C // CH) + 2 * half + 2)
                            for part in range(2):
                                last = nc.tensor.matmul(
                                    xps[:, half * 512:(half + 1) * 512], fw_t[:, k, part],
                                    zt[:, half * 16:(half + 1) * 16, part * MODES:(part + 1) * MODES],
                                    start=(k == 0 and part == 0), stop=(k == WBLK - 1 and part == 1))
                        last.then_inc(modes_done, 1)

                rolled(pe, B, image)

            @block.scalar
            def _(act):
                act.wait_ge(tables_in, 16 * len(loads))
                nc.scalar.activation(eh_hi[:], eh_raw[:], ACT.Copy).then_inc(split_hi, 1)
                for v, (i, scale) in enumerate([(0, 1.0), (0, -1.0), (1, 1.0), (1, 2.0)]):
                    nc.scalar.activation(hmat[:, :, v], hm_raw[:, :, i], ACT.Copy, scale=scale)

                def image(b):
                    for k in range(WBLK):
                        blk = b * WBLK + k
                        for z in range(PER_BLK * ZB):
                            act.wait_ge(z_done, blk * PER_BLK * ZB + z + 1)
                            need(act, modes_done, blk - 1)
                            nc.scalar.activation(zs[:, k % 2, z * SUB:(z + 1) * SUB], zps[z % ZB][:],
                                                 ACT.Copy).then_inc(z_used, 1)
                        for o in range(C // CH):
                            act.wait_ge(t_done, blk * (C // CH) + o + 1)
                            need(act, modes_done, blk)
                            nc.scalar.activation(zt[:, o * CH:(o + 1) * CH], tps[o % 2][:],
                                                 ACT.Copy).then_inc(t_used, 1)
                    act.wait_ge(modes_done, (b + 1) * WBLK)
                    alone(act, passed)
                    nc.scalar.activation(xs[:, b], xps[:], ACT.Copy).then_inc(modes_used, 1)

                rolled(act, B, image)

            @block.vector
            def _(dve):
                dve.wait_ge(split_hi, 1)
                nc.vector.tensor_tensor(eh_lo[:], eh_raw[:], eh_hi[:].bitcast(F32), ALU.subtract)

                def image(b):
                    for i in range(CHUNKS):
                        dve.wait_ge(loaded[i % XRING], 16 * (b * (CHUNKS // XRING) + i // XRING + 1))
                        if i == 0:
                            need(dve, image_merged, b)
                        v = xa[:, i % XRING].rearrange("p t (w c) -> p t w c", c=C)
                        for g in range(GROUPS):
                            last = nc.vector.bn_stats(bn[:, g, i], v[:, :, :, GROUP * g:GROUP * (g + 1)])
                        last.then_inc(chunk_counted, 1)
                    dve.wait_ge(chunk_counted, (b + 1) * CHUNKS)
                    alone(dve, passed)
                    for g in range(GROUPS):
                        last = nc.vector.bn_aggr(merged[:, g], bn[:, g])
                    last.then_inc(image_merged, 1)
                    dve.wait_ge(image_merged, b + 1)
                    nc.vector.tensor_copy(ag[:, b], merged[:])

                rolled(dve, B, image)


def modes_pass(nc, sb, ps, sem, od, ident, ones, onerow, ws_t, wt, xs, ag, mean1, gscale):
    with ExitStack() as mod:
        ot = sb("ot", [RI, B, 2, C, MODES], at=mod)
        prod = sb("prod", [RI, BG, GROUP * MODES], at=mod)
        sx = sb("sx", [RI, B, 4, C], at=mod)
        xt = sb("xt", [P, MODES, B, 4], at=mod)
        wst = sb("wst", [P, MODES, C], at=mod)
        os = sb("os", [P, B * 4, MODES], at=mod)
        m0 = sb("m0", [P, BG], at=mod)
        v0 = sb("v0", [P, BG], at=mod)
        v1 = sb("v1", [P, BG], at=mod)
        root = sb("root", [P, BG], at=mod)
        inv = sb("inv", [P, BG], at=mod)
        r0 = sb("r0", [P, BG], at=mod)
        tmp = sb("tmp", [P, BG], at=mod)
        sxy = sb("sxy", [RI, BG], at=mod)
        syy = sb("syy", [RI, BG], at=mod)
        my = sb("my", [1, BG], at=mod)
        small = ps("small", [P, 512], mod)
        ops = ps("ops", [P, 4, 512], mod)
        ops_t = [ps(f"ops_t{i}", [RI, 512], mod) for i in range(2)]

        link = sem("dve_link")
        sums_in, sums = sem("sums_in"), sem("sums")
        roots_in, roots = sem("roots_in"), sem("roots")
        sx_done, xt_ps, xt_done = sem("sx_done"), sem("xt_ps"), sem("xt_done")
        mixed, os_done = sem("mixed"), sem("os_done")
        back, back_used = sem("back"), sem("back_used")
        modes_out, stored = sem("modes_out"), sem("modes_stored")
        passed = sem("modes_passed")

        TB = 4
        PARTS = MODES // 4
        with nc.Block() as block:
            @block.vector
            def _(dve):
                V = nc.vector
                count = [0]

                def then(ins):
                    count[0] += 1
                    ins.then_inc(link, 1)
                    dve.wait_ge(link, count[0])

                def inverse_root(out, var, step):
                    dve.wait_ge(roots, step)
                    then(V.reciprocal(inv[:], root[:]))
                    then(V.tensor_tensor(tmp[:], inv[:], inv[:], ALU.mult))
                    then(V.tensor_tensor(tmp[:], tmp[:], var[:], ALU.mult))
                    then(V.tensor_scalar(tmp[:], tmp[:], -0.5, 1.5, ALU.mult, ALU.add))
                    then(V.tensor_tensor(out[:], inv[:], tmp[:], ALU.mult))

                dve.wait_ge(sums, 1)
                then(V.tensor_copy(m0[:], small[:, 0:BG]))
                agv = ag[:].rearrange("p b g s -> p (b g) s")
                then(V.tensor_tensor(tmp[:], agv[:, :, 0], m0[:], ALU.subtract))
                then(V.tensor_tensor(tmp[:], tmp[:], tmp[:], ALU.mult))
                V.tensor_tensor(v1[:], tmp[:], agv[:, :, 1], ALU.add).then_inc(sums_in, 1)
                dve.wait_ge(sums, 2)
                V.tensor_scalar(v0[:], small[:, 0:BG], EPS_GN, None, ALU.add).then_inc(roots_in, 1)
                inverse_root(r0, v0, 1)
                dc = xs[0:1].rearrange("r b (g s) p -> r (b g) s p", s=GROUP)[:, :, :, 0]
                then(V.scalar_tensor_tensor(dc, m0[0:1, :, None].to_broadcast([1, BG, GROUP]), -float(H * W), dc,
                                            ALU.mult, ALU.add))
                xv = xs[:].rearrange("r b (g s) p -> r (b g) (s p)", s=GROUP)
                then(V.tensor_tensor(xv, xv, r0[0:RI, :, None].to_broadcast([RI, BG, GROUP * MODES]), ALU.mult))

                def part(s):
                    need(dve, mixed, s)
                    nc.vector.tensor_copy(wst[:], wt[:, s])
                    for b in range(B):
                        last = nc.vector.tensor_copy(
                            sx[:, b], xs[:, b].rearrange("r c (a e) -> r a c e", a=4)[:, :, :, s])
                    last.then_inc(sx_done, 1)

                rolled(dve, PARTS, part)

                dve.wait_ge(back_used, PARTS * TB)
                for i, dst in enumerate((sxy, syy)):
                    for b in range(B):
                        o = ot[:, b, 0].rearrange("r c p -> r (c p)")
                        other = xs[:, b].rearrange("r c p -> r (c p)") if i == 0 else o
                        last = V.tensor_tensor(prod[:, b * GROUPS:(b + 1) * GROUPS].rearrange("r g s -> r (g s)"),
                                               o, other, ALU.mult)
                    then(last)
                    pv = prod[:].rearrange("r g (s p) -> r (g s) p", p=MODES)
                    for row in (0, MODES):
                        last = V.memset(pv[row:row + 1, :, 0], 0.0)
                    then(last)
                    then(V.tensor_reduce(dst[:], prod[:], axis=AX.X, op=ALU.add))
                then(V.tensor_tensor(tmp[:], v0[:], r0[:], ALU.mult))
                then(V.tensor_tensor(sxy[:], sxy[:], tmp[0:RI], ALU.mult))
                oc = ot[0:1, :, 0].rearrange("r b (g s) p -> r b g s p", s=GROUP)[:, :, :, :, 0]
                V.tensor_reduce(my[:].rearrange("r (b g) -> r b g", b=B), oc, axis=AX.X, op=ALU.add).then_inc(sums_in, 1)
                dve.wait_ge(sums, 4)
                then(V.tensor_tensor(tmp[:], v0[:], small[:, 0:BG], ALU.add))
                then(V.tensor_scalar(v1[:], tmp[:], EPS_GN, None, ALU.max))
                V.tensor_tensor(mean1[:], m0[:], ops[:, 0, 0:BG], ALU.add).then_inc(roots_in, 1)
                inverse_root(r0, v1, 2)
                then(V.tensor_tensor(tmp[:], r0[:], r0[:], ALU.mult))
                then(V.tensor_scalar(gscale[:], tmp[:], 1.0 / (4 * 9) ** 2, None, ALU.mult))
                for b in range(B):
                    o1 = ot[0:1, b, 0].rearrange("r (g s) p -> r g s p", s=GROUP)[:, :, :, 0]
                    mb = mean1[0:1, b * GROUPS:(b + 1) * GROUPS, None].to_broadcast([1, GROUPS, GROUP])
                    last = V.scalar_tensor_tensor(o1, mb, -float(H * W), o1, ALU.mult, ALU.add)
                last.then_inc(modes_out, 1)

            @block.scalar
            def _(act):
                act.wait_ge(roots_in, 1)
                nc.scalar.activation(root[:], v0[:], ACT.Sqrt).then_inc(roots, 1)

                def part(s):
                    act.wait_ge(xt_ps, s + 1)
                    xp = small[:].rearrange("p (b r q) -> p r q b", b=B, r=2)
                    for v, (r, scale) in enumerate([(0, 1.0), (1, -1.0), (1, 1.0), (0, 1.0)]):
                        last = nc.scalar.activation(xt[:, :, :, v], xp[:, r], ACT.Copy, scale=scale)
                    last.then_inc(xt_done, 1)
                    act.wait_ge(mixed, s + 1)
                    need(act, back, s * TB)
                    nc.scalar.activation(os[:].rearrange("p v (k q) -> p k q v", k=4),
                                         ops[:, :, 0:256].rearrange("p k (q v) -> p k q v", v=32), ACT.Copy).then_inc(os_done, 1)
                    for i in range(TB):
                        act.wait_ge(back, s * TB + i + 1)
                        o = ot[:].rearrange("r b v d (a e) -> r (b v) a d e", a=4)[:, 4 * i:4 * i + 4, :, :, s]
                        src = ops_t[i % 2][:].rearrange("r (k a d) -> r k a d", k=4, a=4)
                        for k in range(4):
                            last = nc.scalar.activation(o[:, k], src[:, k], ACT.Copy)
                        last.then_inc(back_used, 1)

                rolled(act, PARTS, part)
                act.wait_ge(roots_in, 2)
                nc.scalar.activation(root[:], v1[:], ACT.Sqrt).then_inc(roots, 1)

            @block.tensor
            def _(pe):
                agv = ag[:].rearrange("p b g s -> p (b g) s")
                nc.tensor.matmul(small[:, 0:BG], ones[:], agv[:, :, 0], start=True, stop=True).then_inc(sums, 1)
                pe.wait_ge(sums_in, 1)
                nc.tensor.matmul(small[:, 0:BG], ones[:], v1[:], start=True, stop=True).then_inc(sums, 1)
                pe.wait_ge(roots_in, 1)

                def part(s):
                    pe.wait_ge(sx_done, s + 1)
                    need(pe, xt_done, s)
                    alone(pe, passed)
                    for b in range(B):
                        last = nc.tensor.transpose(small[:, b * RI:(b + 1) * RI],
                                                   sx[:, b].rearrange("r a c -> r (a c)"), ident[0:RI, 0:RI])
                    last.then_inc(xt_ps, 1)
                    pe.wait_ge(xt_done, s + 1)
                    need(pe, os_done, s)
                    alone(pe, passed)
                    for turn in range(4):
                        for q in range(MODES // 4):
                            for a in range(4):
                                k = (turn + a) % 4
                                rows = slice(C * a, C * (a + 1))
                                last = nc.tensor.matmul(
                                    ops[rows, k, q * 32:(q + 1) * 32], wst[rows, k * (MODES // 4) + q],
                                    xt[rows, k * (MODES // 4) + q].rearrange("c b v -> c (b v)"),
                                    start=True, stop=True)
                    last.then_inc(mixed, 1)
                    pe.wait_ge(os_done, s + 1)
                    for i in range(TB):
                        need(pe, back_used, s * TB + i - 1)
                        alone(pe, passed)
                        for k in range(4):
                            b, v = 2 * i + k // 2, k % 2
                            last = nc.tensor.transpose(
                                ops_t[i % 2][:, k * P:(k + 1) * P],
                                os[:, 4 * b + 2 * v:4 * b + 2 * v + 2].rearrange("p r q -> p (r q)"), ident[:])
                        last.then_inc(back, 1)

                rolled(pe, PARTS, part)
                pe.wait_ge(sums_in, 2)
                nc.tensor.matmul(small[:, 0:BG], ws_t[:, 0], sxy[:], start=True, stop=False)
                nc.tensor.matmul(small[:, 0:BG], ws_t[:, 1], syy[:], start=False, stop=True).then_inc(sums, 1)
                nc.tensor.matmul(ops[:, 0, 0:BG], onerow[:], my[:], start=True, stop=True).then_inc(sums, 1)

            @block.sync
            def _(sp):
                sp.wait_ge(modes_out, 1)
                for b in range(B):
                    for twice in range(2):
                        sp.dma_start(od[b, :, twice], ot[:, b].rearrange("r v d p -> r (v d p)")).then_inc(stored, 16)
                sp.wait_ge(stored, 2 * 16 * B)


def gradient_pass(nc, sb, ps, sem, x, out, od, ew_t, eh_hi, eh_lo, hmat, mean1, gscale, eps_t):
    LAG_LO, LAG_GRAD, LAG_SQ, LAG_SUM, LAG_MAG, LAG_OUT = 1, 2, 3, 3, 4, 4
    UNROLL = 4
    with ExitStack() as gr:
        xb = sb("xb", [P, 2, WB, C], at=gr)
        g_t = sb("g_t", [P, 2, C, WB], F32R, at=gr)
        stage = sb("stage", [RI, UNROLL, 4, MODES], at=gr)
        x1 = sb("x1", [P, RING, GROUP, WB], at=gr)
        pr = sb("pr", [P, 2, GROUP, PAIRS + 1], at=gr)
        phi = sb("phi", [P, 2, GROUP, PAIRS + 1], F32R, at=gr)
        plo = sb("plo", [P, 2, GROUP, PAIRS + 1], F32R, at=gr)
        sq = sb("sq", [P, 2, 2, 512], at=gr)
        ssum = sb("ssum", [P, 2, 512], at=gr)
        mag = sb("mag", [P, 2, 512], at=gr)
        ghost = sb("ghost", [P, 4, C], at=gr)
        yps = ps("yps", [P, 2, 512], gr)
        gps = [ps(f"gps{i}", [P, 2, 512], gr) for i in range(2)]
        mps = ps("mps", [P, 512], gr)

        x_in, ghosts, x_out = sem("x_in"), sem("ghosts"), sem("x_out")
        ghost_link = sem("ghost_link")
        y_done, x1_done, pairs_done = sem("y_done"), sem("x1_done"), sem("pairs_done")
        hi_done, lo_done, grad_done = sem("hi_done"), sem("lo_done"), sem("grad_done")
        sq_done, sum_done, mag_done, out_done = sem("sq_done"), sem("sum_done"), sem("mag_done"), sem("out_done")
        staged = [sem(f"staged{i}") for i in range(UNROLL)]
        g_ps, g_hi, g_lo = sem("g_ps"), sem("g_hi"), sem("g_lo")
        passed = sem("gradient_passed")

        def steps(engine, n, emit):
            for k in range(BLOCKS):
                if k == 0 and isinstance(n, int):
                    for g in range(GROUPS):
                        emit(k, g // UNROLL * UNROLL, g % UNROLL)
                    continue
                for j in range(UNROLL):
                    emit(k, 0, j)
                with engine.Fori(1, GROUPS // UNROLL) as i:
                    for j in range(UNROLL):
                        emit(k, i * UNROLL, j)

        class Step:

            def __init__(self, n, k, g0, j, lag=0):
                self.number = n * STEPS + k * GROUPS + g0 + (j - lag)
                if isinstance(g0, int) and g0 + j < lag:
                    k, g0 = k - 1, g0 + GROUPS
                    if k < 0:
                        k, n = BLOCKS - 1, n - 1
                self.exists = k < BLOCKS and not (isinstance(n, int) and n < 0)
                if self.exists:
                    self.turn, self.block, self.rows = n, k, ROWS[k]
                    self.slot = (n + k) % 2
                    self.g = g0 + (j - lag)
                    self.ring = (g0 + (j - lag + RING)) % RING
                    self.two = (j - lag) % 2

        SPREAD = (1, 2)

        with nc.Block() as block:
            @block.sync
            def _(sp):
                def load(n, k):
                    n1, k1 = (n, k) if k < BLOCKS else (n + 1, k - BLOCKS)
                    r0, rows = ROW0[k1], ROWS[k1]
                    half = n1 // B
                    src = x[n1 % B, r0:r0 + rows, bass.ds(half * (W - WIN), WIN), :]
                    sp.dma_start(xb[0:rows, (n1 + k1) % 2, bass.ds(half * -2 + 2, WIN), :], src).then_inc(x_in, 16)

                def store(n, k):
                    first, last = OUT[k]
                    at = 0
                    for a, z in ((first, first + (last - first) // 16 * 16), (first + (last - first) // 16 * 16, last)):
                        if a < z:
                            r = a - ROW0[k]
                            sp.dma_start(out[n % B, a:z, bass.ds((n // B) * HALF, HALF), :],
                                         xb[r:r + z - a, (n + k) % 2, 2:2 + HALF, :]).then_inc(x_out, 16)

                pieces = [2 if (z - a) % 16 and (z - a) >= 16 else 1 for a, z in OUT]
                per_turn = sum(pieces)

                def turn(n, last=False):
                    for k in range(BLOCKS):
                        sp.wait_ge(out_done, n * STEPS + (k + 1) * GROUPS)
                        store(n, k)
                        if last and k + 2 >= BLOCKS:
                            continue
                        sp.wait_ge(x_out, 16 * (n * per_turn + sum(pieces[:k + 1])))
                        sp.wait_ge(x_in, 16 * (n * BLOCKS + k + 2))
                        load(n, k + 2)

                load(0, 0)
                sp.wait_ge(x_in, 16)
                load(0, 1)
                with sp.Fori(0, TURNS - 1) as n:
                    turn(n)
                turn(TURNS - 1, last=True)
                sp.wait_ge(x_out, 16 * TURNS * per_turn)

            @block.gpsimd
            def _(pool):
                G = nc.gpsimd
                def fetch(m, i, slot):
                    need(pool, g_ps, (m * (C // UNROLL) + i - 1) * UNROLL + slot + 1)
                    src = od[m % B].rearrange("r t (v d p) -> r (t v) d p", v=2, d=C)[:, :, bass.ds(i * UNROLL + slot, 1), :]
                    pool.dma_start(stage[:, slot], src.rearrange("r v d p -> r v (d p)")).then_inc(staged[slot], 16)

                def ghosts_of(n, k):
                    rows, slot, half = ROWS[k], (n + k) % 2, n // B
                    unit = n * BLOCKS + k
                    pool.wait_ge(x_in, 16 * (unit + 1))

                    def col(left, right):
                        return xb[0:rows, slot, bass.ds(half * (right - left) + left, 1), :].rearrange("p w c -> p (w c)")
                    edge, inner = col(2, WIN - 1), col(3, WIN - 2)
                    near, far = col(1, WIN), col(0, WIN + 1)
                    def then(step, ins):
                        ins.then_inc(ghost_link, 1)
                        pool.wait_ge(ghost_link, 4 * unit + step + 1)
                        alone(pool, passed)

                    alone(pool, passed)
                    then(0, G.tensor_tensor(ghost[0:rows, 0], edge, inner, ALU.add))
                    then(1, G.tensor_scalar(ghost[0:rows, 1], ghost[0:rows, 0], 0.5, None, ALU.mult))
                    G.tensor_copy(near, ghost[0:rows, 1])
                    then(2, G.tensor_tensor(ghost[0:rows, 2], edge, ghost[0:rows, 1], ALU.add))
                    then(3, G.tensor_scalar(ghost[0:rows, 3], ghost[0:rows, 2], -1.0, None, ALU.mult))
                    G.tensor_copy(far, ghost[0:rows, 3]).then_inc(ghosts, 1)

                def fetches(m, first, count):
                    with pool.Fori(first, first + count) as i:
                        for slot in range(UNROLL):
                            fetch(m, i, slot)

                for slot in range(UNROLL):
                    fetch(0, 0, slot)
                fetches(0, 1, C // UNROLL - 1)
                ghosts_of(0, 0)

                def turn(n, last=False):
                    for k in range(BLOCKS):
                        if k in SPREAD:
                            fetches(n + 1, (k - SPREAD[0]) * (GROUPS // UNROLL), GROUPS // UNROLL)
                        if not (last and k == BLOCKS - 1):
                            ghosts_of(n + (k + 1) // BLOCKS, (k + 1) % BLOCKS)

                with pool.Fori(0, TURNS - 1) as n:
                    turn(n)
                turn(TURNS - 1, last=True)

            @block.tensor
            def _(pe):
                T = nc.tensor

                def spread(m, i, slot):
                    pe.wait_ge(staged[slot], 16 * (m * (C // UNROLL) + i + 1))
                    need(pe, g_lo, (m * (C // UNROLL) + i) * UNROLL + slot)
                    alone(pe, passed)
                    modes = stage[:, slot].rearrange("r v p -> r (v p)")
                    half = ew_t[:, bass.ds(m // B % 2, 1), :].rearrange("r h w -> r (h w)")
                    T.matmul(mps[:, 0:WB], modes, half, start=True, stop=True).then_inc(g_ps, 1)

                def y(s):
                    need(pe, x1_done, s.number)
                    alone(pe, passed)
                    for ch in range(GROUP):
                        rhs = g_t[:, s.turn % 2, bass.ds(s.g * GROUP + ch, 1), :].rearrange("p c w -> p (c w)")
                        T.matmul(yps[0:s.rows, ch, 0:WB], eh_lo[:, s.block, 0:s.rows], rhs, start=True, stop=False)
                        last = T.matmul(yps[0:s.rows, ch, 0:WB], eh_hi[:, s.block, 0:s.rows], rhs, start=False, stop=True)
                    last.then_inc(y_done, 1)

                def grad(s):
                    if not s.exists:
                        return
                    pe.wait_ge(lo_done, s.number + 1)
                    need(pe, sq_done, s.number - 1)
                    rows, v = s.rows, VARIANT[s.block]
                    taps = [[(0, 0), (1, 3)], [(2, 0), (3, 1), (3, 2), (2, 3)]]
                    for d in range(2):
                        todo = [(m, w, part) for m, w in taps[d] for part in (plo, phi)]
                        for i, (m, w, part) in enumerate(todo):
                            last = T.matmul(gps[s.two][:, d], hmat[0:rows, v, m],
                                            part[0:rows, s.two, :, w:w + HALF],
                                            start=(i == 0), stop=(i == len(todo) - 1))
                    last.then_inc(grad_done, 1)

                for slot in range(UNROLL):
                    spread(0, 0, slot)
                with pe.Fori(1, C // UNROLL) as i:
                    for slot in range(UNROLL):
                        spread(0, i, slot)

                def turn(n):
                    def emit(k, g0, j):
                        if k == 0 and isinstance(g0, int) and j == 0:
                            pe.wait_ge(g_lo, (n + 1) * C)
                        y(Step(n, k, g0, j))
                        grad(Step(n, k, g0, j, LAG_GRAD))
                        if k in SPREAD:
                            spread(n + 1, (k - SPREAD[0]) * (GROUPS // UNROLL) + g0 // UNROLL, j)
                    steps(pe, n, emit)

                rolled(pe, TURNS, turn)
                for j in range(LAG_GRAD):
                    grad(Step(TURNS - 1, BLOCKS, 0, j, LAG_GRAD))

            @block.scalar
            def _(act):
                A = nc.scalar

                def high(m, c):
                    act.wait_ge(g_ps, m * C + c + 1)
                    alone(act, passed)
                    dst = g_t[:, m % 2, bass.ds(c, 1), :].rearrange("p c w -> p (c w)")
                    A.activation(dst, mps[:, 0:WB], ACT.Copy).then_inc(g_hi, 1)

                def magnitude(s):
                    if not s.exists:
                        return
                    act.wait_ge(sum_done, s.number + 1)
                    need(act, out_done, s.number - 1)
                    alone(act, passed)
                    r = slice(0, s.rows)
                    scale = gscale[r, bass.ds(s.turn % B * GROUPS + s.g, 1)]
                    A.activation(mag[r, s.two], ssum[r, s.two], ACT.Sqrt, bias=eps_t[r], scale=scale).then_inc(mag_done, 1)

                def squares(s):
                    if not s.exists:
                        return
                    act.wait_ge(grad_done, s.number + 1)
                    need(act, sum_done, s.number - 1)
                    r = slice(0, s.rows)
                    A.activation(sq[r, s.two], gps[s.two][r], ACT.Square).then_inc(sq_done, 1)

                def high_pairs(s):
                    act.wait_ge(pairs_done, s.number + 1)
                    need(act, grad_done, s.number - 1)
                    r = slice(0, s.rows)
                    A.activation(phi[r, s.two, :, 0:PAIRS], pr[r, s.two, :, 0:PAIRS], ACT.Copy).then_inc(hi_done, 1)

                with act.Fori(0, C) as c:
                    high(0, c)

                def turn(n):
                    def emit(k, g0, j):
                        magnitude(Step(n, k, g0, j, LAG_MAG))
                        squares(Step(n, k, g0, j, LAG_SQ))
                        high_pairs(Step(n, k, g0, j))
                        if k in SPREAD:
                            high(n + 1, (k - SPREAD[0]) * GROUPS + g0 + j)
                    steps(act, n, emit)

                rolled(act, TURNS, turn)
                for j in range(LAG_MAG):
                    magnitude(Step(TURNS - 1, BLOCKS, 0, j, LAG_MAG))
                    if j < LAG_SQ:
                        squares(Step(TURNS - 1, BLOCKS, 0, j, LAG_SQ))

            @block.vector
            def _(dve):
                V = nc.vector

                def low(m, c):
                    dve.wait_ge(g_hi, m * C + c + 1)
                    dst = g_t[RI:P, m % 2, bass.ds(c, 1), :].rearrange("p c w -> p (c w)")
                    V.tensor_tensor(dst, mps[RI:P, 0:WB], dst.bitcast(F32), ALU.subtract).then_inc(g_lo, 1)

                def add_y(s):
                    dve.wait_ge(y_done, s.number + 1)
                    r = slice(0, s.rows)
                    src = xb[r, s.slot, :, bass.ds(s.g * GROUP, GROUP)].rearrange("p w c -> p c w")
                    V.tensor_tensor(x1[r, s.ring], src, yps[r, :, 0:WB], ALU.add).then_inc(x1_done, 1)

                def low_pairs(s):
                    if not s.exists:
                        return
                    dve.wait_ge(hi_done, s.number + 1)
                    need(dve, grad_done, s.number - 1)
                    r = slice(0, s.rows)
                    V.tensor_tensor(plo[r, s.two, :, 0:PAIRS], pr[r, s.two, :, 0:PAIRS],
                                    phi[r, s.two, :, 0:PAIRS].bitcast(F32), ALU.subtract).then_inc(lo_done, 1)

                def pairs(s):
                    dve.wait_ge(x1_done, s.number + 1)
                    r = slice(0, s.rows)
                    V.tensor_tensor(pr[r, s.two, :, 0:PAIRS], x1[r, s.ring, :, 0:PAIRS],
                                    x1[r, s.ring, :, 1:WB], ALU.add).then_inc(pairs_done, 1)

                def add_squares(s):
                    if not s.exists:
                        return
                    dve.wait_ge(sq_done, s.number + 1)
                    need(dve, mag_done, s.number - 1)
                    r = slice(0, s.rows)
                    V.tensor_tensor(ssum[r, s.two], sq[r, s.two, 0], sq[r, s.two, 1], ALU.add).then_inc(sum_done, 1)

                def result(s):
                    if not s.exists:
                        return
                    dve.wait_ge(mag_done, s.number + 1)
                    r = slice(0, s.rows)
                    dst = xb[r, s.slot, 2:2 + HALF, bass.ds(s.g * GROUP, GROUP)].rearrange("p w c -> p c w")
                    V.scalar_tensor_tensor(dst, x1[r, s.ring, :, 2:2 + HALF],
                                           mean1[r, bass.ds(s.turn % B * GROUPS + s.g, 1)],
                                           mag[r, s.two].rearrange("p (c w) -> p c w", c=GROUP),
                                           ALU.add, ALU.add).then_inc(out_done, 1)

                with dve.Fori(0, C) as c:
                    low(0, c)

                def turn(n):
                    def emit(k, g0, j):
                        if isinstance(g0, int) and j == 0:
                            dve.wait_ge(ghosts, n * BLOCKS + k + 1)
                        add_y(Step(n, k, g0, j))
                        low_pairs(Step(n, k, g0, j, LAG_LO))
                        pairs(Step(n, k, g0, j))
                        add_squares(Step(n, k, g0, j, LAG_SUM))
                        result(Step(n, k, g0, j, LAG_OUT))
                        if k in SPREAD:
                            low(n + 1, (k - SPREAD[0]) * GROUPS + g0 + j)
                    steps(dve, n, emit)

                rolled(dve, TURNS, turn)
                for j in range(LAG_OUT):
                    if j < LAG_LO:
                        low_pairs(Step(TURNS - 1, BLOCKS, 0, j, LAG_LO))
                    if j < LAG_SUM:
                        add_squares(Step(TURNS - 1, BLOCKS, 0, j, LAG_SUM))
                    result(Step(TURNS - 1, BLOCKS, 0, j, LAG_OUT))


def kernel(x, L0_conv_W):
    import concourse.bacc as bacc
    from concourse.bass_utils import run_bass_kernel_spmd

    nc = bacc.Bacc("TRN2", target_bir_lowering=False, num_devices=1)
    tab = tables()
    arrays = {"x_dram": np.ascontiguousarray(x), "w_dram": np.ascontiguousarray(L0_conv_W)}
    arrays.update({f"{n}_dram": a for n, a in tab.items()})
    aps = {n: nc.dram_tensor(n, a.shape, mybir.dt.from_np(a.dtype), kind="ExternalInput").ap()
           for n, a in arrays.items()}
    out = nc.dram_tensor("out_dram", (B, H, W, C), F32, kind="ExternalOutput").ap()
    od = nc.dram_tensor("mixed_modes", (B, RI, 2, 2 * C * MODES), F32, kind="Internal").ap()
    spectral_gradient_kernel(nc, aps["x_dram"], aps["w_dram"], {n: aps[f"{n}_dram"] for n in tab}, out, od)
    r = run_bass_kernel_spmd(nc, [arrays], core_ids=[0])
    return r.results[0]["out_dram"]
```

```python
from contextlib import ExitStack

import numpy as np

import concourse.bass as bass
from concourse import mybir

F32 = mybir.dt.float32
F32R = mybir.dt.float32r
ALU = mybir.AluOpType
ACT = mybir.ActivationFunctionType
AX = mybir.AxisListType

B, H, W, C = 8, 512, 512, 32
N = 512
MODES = 32
GROUP = 2
GROUPS = C // GROUP
BG = B * GROUPS
P = 128
RI = 2 * MODES
EPS_GN = 1e-5
EPS_GRAD = 1e-6

HALF = W // 2
WIN = HALF + 2
WB = WIN + 2
PAIRS = WB - 1
ROW0 = [0, 124, 248, 372]
OUT = [(0, 126), (126, 250), (250, 374), (374, 498)]
BLOCKS = len(ROW0)
STRIP = P // B
STRIP0 = H - STRIP
VARIANT = [0, 1, 1, 1]
TURNS = 2 * B
STEPS = BLOCKS * GROUPS
RING = 8

CW = 32
CHUNKS = W // CW
HB = H // P
XRING = 4
WBLK = W // P
PER_BLK = P // CW
SUB = 512 // C


def tables():
    k = np.arange(MODES)
    ang = 2 * np.pi * np.outer(np.arange(N), k) / N
    cos, sin = np.cos(ang), np.sin(ang)
    fh = np.concatenate([cos, -sin], 1).reshape(HB, P, RI).transpose(1, 0, 2)
    fw = np.stack([np.concatenate([cos, -sin], 1), np.concatenate([sin, cos], 1)], 1)
    fw = fw.reshape(WBLK, P, 2, RI).transpose(1, 0, 2, 3)
    alpha = np.where(k == 0, 1.0, 2.0)
    rows = np.concatenate([cos * alpha, sin * alpha], 1).T / N
    left = np.concatenate([-(1.5 * rows[:, :1] + 0.5 * rows[:, 1:2]), 0.5 * (rows[:, :1] + rows[:, 1:2]),
                           rows[:, :WIN]], 1)
    right = np.concatenate([rows[:, W - WIN:], 0.5 * (rows[:, -1:] + rows[:, -2:-1]),
                            -(1.5 * rows[:, -1:] + 0.5 * rows[:, -2:-1])], 1)
    ew = np.stack([left, right], 1)
    both = np.tile(np.concatenate([cos, -sin], 1).T / N, (2, 1))
    eh = np.concatenate([both[:, r0:r0 + P] for r0 in ROW0] + [both[:, STRIP0:]], 1)
    pool = sum(np.eye(H, k=d) for d in (-1, 0, 1))
    pool[0] *= 1.5
    pool[-1] *= 1.5
    smooth = (2 * np.eye(H) + np.eye(H, k=1) + np.eye(H, k=-1)) @ pool
    diff = (np.eye(H, k=-1) - np.eye(H, k=1)) @ pool
    hm = np.zeros((P, 3, 2, P))
    for i, m in enumerate((smooth, diff)):
        for v, r0 in enumerate(ROW0[:2]):
            hm[:, v, i] = m[r0:r0 + P, r0:r0 + P].T
        hm[:, 2, i] = np.kron(np.eye(B), m[STRIP0:, STRIP0:].T)
    sign = np.concatenate([alpha, -alpha])
    beta = np.where(k == 0, 0.5, 2.0)
    ws = np.stack([2 * sign, np.concatenate([beta, beta])], 1) / N**2 / (GROUP * H * W)
    ws = np.repeat(ws[:, :, None], P, 2)
    t = {"fh": fh, "fw": fw, "ew": ew, "eh": eh, "hm": hm, "ws": ws, "ones": np.full((P, P), 1 / P),
         "onerow": np.full((1, P), 1 / (GROUP * N**2)), "ident": np.eye(P), "owner": np.kron(np.eye(B), np.ones((STRIP, 1)))}
    return {n: np.ascontiguousarray(a, np.float32) for n, a in t.items()}


def spectral_gradient_kernel(nc, x, w_modes, tab, out, od, strip_y):
    ctx = ExitStack()
    with ctx:
        def sb(name, shape, dt=F32, at=ctx):
            return at.enter_context(nc.sbuf_tensor(name, shape, dt))

        def ps(name, shape, at):
            return at.enter_context(nc.psum_tensor(name, shape, F32))

        def sem(name):
            return ctx.enter_context(nc.semaphore(name))

        ew_t = sb("ew_t", [RI, 2, WB])
        eh_hi = sb("eh_hi", [P, BLOCKS * P + STRIP], F32R)
        eh_lo = sb("eh_lo", [P, BLOCKS * P + STRIP], F32R)
        hmat = sb("hmat", [P, 3, 4, P], F32R)
        mean1 = sb("mean1", [P, BG])
        gscale = sb("gscale", [P, BG])
        strip_mean = sb("strip_mean", [P, GROUPS])
        strip_scale = sb("strip_scale", [P, GROUPS])
        eps_t = sb("eps_t", [P, 1])

        spectra = ExitStack()
        with spectra:
            fh_t = sb("fh_t", [P, HB, RI], at=spectra)
            fw_t = sb("fw_t", [P, WBLK, 2, RI], at=spectra)
            ident = sb("ident_t", [P, P], at=spectra)
            ones = sb("ones_t", [P, P], at=spectra)
            onerow = sb("onerow_t", [1, P], at=spectra)
            owner = sb("owner_t", [P, B], at=spectra)
            ws_t = sb("ws_t", [RI, 2, P], at=spectra)
            wt = sb("wt", [P, MODES // 4, MODES, C], at=spectra)
            xs = sb("xs", [RI, B, C, MODES], at=spectra)
            ag = sb("ag", [P, B, GROUPS, 2], at=spectra)
            forward_pass(nc, sb, ps, sem, x, w_modes, tab, fh_t, fw_t, ident, ones, onerow, owner, ws_t, wt, xs, ag,
                         ew_t, eh_hi, eh_lo, hmat, eps_t)
            modes_pass(nc, sb, ps, sem, od, ident, ones, onerow, owner, ws_t, wt, xs, ag, mean1, gscale,
                       strip_mean, strip_scale)
        gradient_pass(nc, sb, ps, sem, x, out, od, strip_y, ew_t, eh_hi, eh_lo, hmat, mean1, gscale,
                      strip_mean, strip_scale, eps_t)


def need(engine, semaphore, count):
    if not (isinstance(count, int) and count <= 0):
        engine.wait_ge(semaphore, count)


def alone(engine, passed):
    engine.sem_inc(passed, 1)


def rolled(engine, count, body):
    body(0)
    with engine.Fori(1, count) as i:
        body(i)


def forward_pass(nc, sb, ps, sem, x, w_modes, tab, fh_t, fw_t, ident, ones, onerow, owner, ws_t, wt, xs, ag,
                 ew_t, eh_hi, eh_lo, hmat, eps_t):
    with ExitStack() as fwd:
        xa = sb("xa", [P, XRING, HB, CW * C], at=fwd)
        zs = sb("zs", [RI, 2, P, C], at=fwd)
        zt = sb("zt", [P, C, RI], at=fwd)
        bn = sb("bn", [P, GROUPS, CHUNKS, 6], at=fwd)
        merged = sb("merged", [P, GROUPS, 2], at=fwd)
        eh_raw = sb("eh_raw", [P, BLOCKS * P + STRIP], at=fwd)
        hm_raw = sb("hm_raw", [P, 3, 2, P], at=fwd)
        zps = [ps(f"zps{i}", [RI, 512], fwd) for i in range(2)]
        tps = [ps(f"tps{i}", [P, 512], fwd) for i in range(2)]
        xps = ps("xps", [RI, C * MODES], fwd)

        loaded = [sem(f"chunk_loaded{i}") for i in range(XRING)]
        tables_in, weights_in = sem("tables_in"), sem("weights_in")
        chunk_counted = sem("chunk_counted")
        z_done, z_used = sem("z_done"), sem("z_used")
        t_done, t_used = sem("t_done"), sem("t_used")
        modes_done, modes_used = sem("modes_done"), sem("modes_used")
        split_hi, split_lo = sem("split_hi"), sem("split_lo")
        image_merged, passed = sem("image_merged"), sem("forward_passed")

        loads = [(fh_t, "fh"), (fw_t, "fw"), (ident, "ident"), (ones, "ones"), (onerow, "onerow"), (owner, "owner"), (ws_t, "ws"),
                 (ew_t, "ew"), (eh_raw, "eh"), (hm_raw, "hm")]
        x_v = x.rearrange("b (t p) w c -> b p t (w c)", p=P)
        w_v = w_modes.rearrange("(r s) q c d -> r c s q d", r=4)
        CH = 512 // RI
        ZB = CW // SUB

        with nc.Block() as block:
            @block.sync
            def _(sp):
                for t, name in loads:
                    sp.dma_start(t[:], tab[name]).then_inc(tables_in, 16)

                def ring(i):
                    for j in range(XRING):
                        need(sp, z_done, ((i - 1) * XRING + j + 1) * ZB)
                        need(sp, chunk_counted, (i - 1) * XRING + j + 1)
                        at = (i * XRING + j) % CHUNKS * (CW * C)
                        sp.dma_start(xa[:, j], x_v[i * XRING // CHUNKS, :, :, bass.ds(at, CW * C)]
                                     ).then_inc(loaded[j], 16)

                rolled(sp, B * CHUNKS // XRING, ring)

            @block.gpsimd
            def _(pool):
                nc.gpsimd.memset(eps_t[:], EPS_GRAD)
                for r in range(4):
                    for s in range(MODES // 4):
                        pool.dma_start(wt[r * C:(r + 1) * C, s], w_v[r, :, s]).then_inc(weights_in, 16)
                pool.wait_ge(weights_in, 16 * MODES)

            @block.tensor
            def _(pe):
                pe.wait_ge(tables_in, 16 * len(loads))

                def image(b):
                    for k in range(WBLK):
                        blk = b * WBLK + k
                        for j in range(PER_BLK):
                            chunk = blk * PER_BLK + j
                            pe.wait_ge(loaded[j], 16 * (blk + 1))
                            for s in range(ZB):
                                need(pe, z_used, (chunk - 1) * ZB + s + 1)
                                for t in range(HB):
                                    last = nc.tensor.matmul(
                                        zps[s][:], fh_t[:, t], xa[:, j, t, s * 512:(s + 1) * 512],
                                        start=(t == 0), stop=(t == HB - 1))
                                last.then_inc(z_done, 1)
                        pe.wait_ge(z_used, (blk + 1) * PER_BLK * ZB)
                        for o in range(C // CH):
                            need(pe, t_used, blk * (C // CH) + o - 1)
                            alone(pe, passed)
                            for c in range(CH):
                                last = nc.tensor.transpose(tps[o % 2][:, c * RI:(c + 1) * RI],
                                                           zs[:, k % 2, :, o * CH + c], ident[0:RI, 0:RI])
                            last.then_inc(t_done, 1)
                        if k == 0:
                            need(pe, modes_used, b)
                        for half in range(2):
                            pe.wait_ge(t_used, blk * (C // CH) + 2 * half + 2)
                            for part in range(2):
                                last = nc.tensor.matmul(
                                    xps[:, half * 512:(half + 1) * 512], fw_t[:, k, part],
                                    zt[:, half * 16:(half + 1) * 16, part * MODES:(part + 1) * MODES],
                                    start=(k == 0 and part == 0), stop=(k == WBLK - 1 and part == 1))
                        last.then_inc(modes_done, 1)

                rolled(pe, B, image)

            @block.scalar
            def _(act):
                act.wait_ge(tables_in, 16 * len(loads))
                nc.scalar.activation(eh_hi[:], eh_raw[:], ACT.Copy).then_inc(split_hi, 1)
                for v, (i, scale) in enumerate([(0, 1.0), (0, -1.0), (1, 1.0), (1, 2.0)]):
                    nc.scalar.activation(hmat[:, :, v], hm_raw[:, :, i], ACT.Copy, scale=scale)

                def image(b):
                    for k in range(WBLK):
                        blk = b * WBLK + k
                        for z in range(PER_BLK * ZB):
                            act.wait_ge(z_done, blk * PER_BLK * ZB + z + 1)
                            need(act, modes_done, blk - 1)
                            nc.scalar.activation(zs[:, k % 2, z * SUB:(z + 1) * SUB], zps[z % ZB][:],
                                                 ACT.Copy).then_inc(z_used, 1)
                        for o in range(C // CH):
                            act.wait_ge(t_done, blk * (C // CH) + o + 1)
                            need(act, modes_done, blk)
                            nc.scalar.activation(zt[:, o * CH:(o + 1) * CH], tps[o % 2][:],
                                                 ACT.Copy).then_inc(t_used, 1)
                    act.wait_ge(modes_done, (b + 1) * WBLK)
                    alone(act, passed)
                    nc.scalar.activation(xs[:, b], xps[:], ACT.Copy).then_inc(modes_used, 1)

                rolled(act, B, image)

            @block.vector
            def _(dve):
                dve.wait_ge(split_hi, 1)
                nc.vector.tensor_tensor(eh_lo[:], eh_raw[:], eh_hi[:].bitcast(F32), ALU.subtract)

                def image(b):
                    for i in range(CHUNKS):
                        dve.wait_ge(loaded[i % XRING], 16 * (b * (CHUNKS // XRING) + i // XRING + 1))
                        if i == 0:
                            need(dve, image_merged, b)
                        v = xa[:, i % XRING].rearrange("p t (w c) -> p t w c", c=C)
                        for g in range(GROUPS):
                            last = nc.vector.bn_stats(bn[:, g, i], v[:, :, :, GROUP * g:GROUP * (g + 1)])
                        last.then_inc(chunk_counted, 1)
                    dve.wait_ge(chunk_counted, (b + 1) * CHUNKS)
                    alone(dve, passed)
                    for g in range(GROUPS):
                        last = nc.vector.bn_aggr(merged[:, g], bn[:, g])
                    last.then_inc(image_merged, 1)
                    dve.wait_ge(image_merged, b + 1)
                    nc.vector.tensor_copy(ag[:, b], merged[:])

                rolled(dve, B, image)


def modes_pass(nc, sb, ps, sem, od, ident, ones, onerow, owner, ws_t, wt, xs, ag, mean1, gscale,
               strip_mean, strip_scale):
    with ExitStack() as mod:
        ot = sb("ot", [RI, B, 2, C, MODES], at=mod)
        prod = sb("prod", [RI, BG, GROUP * MODES], at=mod)
        sx = sb("sx", [RI, B, 4, C], at=mod)
        xt = sb("xt", [P, MODES, B, 4], at=mod)
        wst = sb("wst", [P, MODES, C], at=mod)
        os = sb("os", [P, B * 4, MODES], at=mod)
        m0 = sb("m0", [P, BG], at=mod)
        v0 = sb("v0", [P, BG], at=mod)
        v1 = sb("v1", [P, BG], at=mod)
        root = sb("root", [P, BG], at=mod)
        inv = sb("inv", [P, BG], at=mod)
        r0 = sb("r0", [P, BG], at=mod)
        tmp = sb("tmp", [P, BG], at=mod)
        sxy = sb("sxy", [RI, BG], at=mod)
        syy = sb("syy", [RI, BG], at=mod)
        my = sb("my", [1, BG], at=mod)
        small = ps("small", [P, 512], mod)
        ops = ps("ops", [P, 4, 512], mod)
        ops_t = [ps(f"ops_t{i}", [RI, 512], mod) for i in range(2)]

        link = sem("dve_link")
        sums_in, sums = sem("sums_in"), sem("sums")
        roots_in, roots = sem("roots_in"), sem("roots")
        sx_done, xt_ps, xt_done = sem("sx_done"), sem("xt_ps"), sem("xt_done")
        mixed, os_done = sem("mixed"), sem("os_done")
        back, back_used = sem("back"), sem("back_used")
        modes_out, stored = sem("modes_out"), sem("modes_stored")
        passed = sem("modes_passed")

        TB = 4
        PARTS = MODES // 4
        with nc.Block() as block:
            @block.vector
            def _(dve):
                V = nc.vector
                count = [0]

                def then(ins):
                    count[0] += 1
                    ins.then_inc(link, 1)
                    dve.wait_ge(link, count[0])

                def inverse_root(out, var, step):
                    dve.wait_ge(roots, step)
                    then(V.reciprocal(inv[:], root[:]))
                    then(V.tensor_tensor(tmp[:], inv[:], inv[:], ALU.mult))
                    then(V.tensor_tensor(tmp[:], tmp[:], var[:], ALU.mult))
                    then(V.tensor_scalar(tmp[:], tmp[:], -0.5, 1.5, ALU.mult, ALU.add))
                    then(V.tensor_tensor(out[:], inv[:], tmp[:], ALU.mult))

                dve.wait_ge(sums, 1)
                then(V.tensor_copy(m0[:], small[:, 0:BG]))
                agv = ag[:].rearrange("p b g s -> p (b g) s")
                then(V.tensor_tensor(tmp[:], agv[:, :, 0], m0[:], ALU.subtract))
                then(V.tensor_tensor(tmp[:], tmp[:], tmp[:], ALU.mult))
                V.tensor_tensor(v1[:], tmp[:], agv[:, :, 1], ALU.add).then_inc(sums_in, 1)
                dve.wait_ge(sums, 2)
                V.tensor_scalar(v0[:], small[:, 0:BG], EPS_GN, None, ALU.add).then_inc(roots_in, 1)
                inverse_root(r0, v0, 1)
                dc = xs[0:1].rearrange("r b (g s) p -> r (b g) s p", s=GROUP)[:, :, :, 0]
                then(V.scalar_tensor_tensor(dc, m0[0:1, :, None].to_broadcast([1, BG, GROUP]), -float(H * W), dc,
                                            ALU.mult, ALU.add))
                xv = xs[:].rearrange("r b (g s) p -> r (b g) (s p)", s=GROUP)
                then(V.tensor_tensor(xv, xv, r0[0:RI, :, None].to_broadcast([RI, BG, GROUP * MODES]), ALU.mult))

                def part(s):
                    need(dve, mixed, s)
                    nc.vector.tensor_copy(wst[:], wt[:, s])
                    for b in range(B):
                        last = nc.vector.tensor_copy(
                            sx[:, b], xs[:, b].rearrange("r c (a e) -> r a c e", a=4)[:, :, :, s])
                    last.then_inc(sx_done, 1)

                rolled(dve, PARTS, part)

                dve.wait_ge(back_used, PARTS * TB)
                for i, dst in enumerate((sxy, syy)):
                    for b in range(B):
                        o = ot[:, b, 0].rearrange("r c p -> r (c p)")
                        other = xs[:, b].rearrange("r c p -> r (c p)") if i == 0 else o
                        last = V.tensor_tensor(prod[:, b * GROUPS:(b + 1) * GROUPS].rearrange("r g s -> r (g s)"),
                                               o, other, ALU.mult)
                    then(last)
                    pv = prod[:].rearrange("r g (s p) -> r (g s) p", p=MODES)
                    for row in (0, MODES):
                        last = V.memset(pv[row:row + 1, :, 0], 0.0)
                    then(last)
                    then(V.tensor_reduce(dst[:], prod[:], axis=AX.X, op=ALU.add))
                then(V.tensor_tensor(tmp[:], v0[:], r0[:], ALU.mult))
                then(V.tensor_tensor(sxy[:], sxy[:], tmp[0:RI], ALU.mult))
                oc = ot[0:1, :, 0].rearrange("r b (g s) p -> r b g s p", s=GROUP)[:, :, :, :, 0]
                V.tensor_reduce(my[:].rearrange("r (b g) -> r b g", b=B), oc, axis=AX.X, op=ALU.add).then_inc(sums_in, 1)
                dve.wait_ge(sums, 4)
                then(V.tensor_tensor(tmp[:], v0[:], small[:, 0:BG], ALU.add))
                then(V.tensor_scalar(v1[:], tmp[:], EPS_GN, None, ALU.max))
                V.tensor_tensor(mean1[:], m0[:], ops[:, 0, 0:BG], ALU.add).then_inc(roots_in, 1)
                inverse_root(r0, v1, 2)
                then(V.tensor_tensor(tmp[:], r0[:], r0[:], ALU.mult))
                then(V.tensor_scalar(gscale[:], tmp[:], 1.0 / (4 * 9) ** 2, None, ALU.mult))
                own = owner[:, :, None].to_broadcast([P, B, GROUPS])
                for src, dst in ((mean1, strip_mean), (gscale, strip_scale)):
                    then(V.tensor_tensor(tmp[:].rearrange("p (b g) -> p b g", b=B),
                                         src[:].rearrange("p (b g) -> p b g", b=B), own, ALU.mult))
                    then(V.tensor_reduce(dst[:], tmp[:].rearrange("p (b g) -> p g b", b=B), axis=AX.X, op=ALU.add))
                for b in range(B):
                    o1 = ot[0:1, b, 0].rearrange("r (g s) p -> r g s p", s=GROUP)[:, :, :, 0]
                    mb = mean1[0:1, b * GROUPS:(b + 1) * GROUPS, None].to_broadcast([1, GROUPS, GROUP])
                    last = V.scalar_tensor_tensor(o1, mb, -float(H * W), o1, ALU.mult, ALU.add)
                last.then_inc(modes_out, 1)

            @block.scalar
            def _(act):
                act.wait_ge(roots_in, 1)
                nc.scalar.activation(root[:], v0[:], ACT.Sqrt).then_inc(roots, 1)

                def part(s):
                    act.wait_ge(xt_ps, s + 1)
                    xp = small[:].rearrange("p (b r q) -> p r q b", b=B, r=2)
                    for v, (r, scale) in enumerate([(0, 1.0), (1, -1.0), (1, 1.0), (0, 1.0)]):
                        last = nc.scalar.activation(xt[:, :, :, v], xp[:, r], ACT.Copy, scale=scale)
                    last.then_inc(xt_done, 1)
                    act.wait_ge(mixed, s + 1)
                    need(act, back, s * TB)
                    nc.scalar.activation(os[:].rearrange("p v (k q) -> p k q v", k=4),
                                         ops[:, :, 0:256].rearrange("p k (q v) -> p k q v", v=32), ACT.Copy).then_inc(os_done, 1)
                    for i in range(TB):
                        act.wait_ge(back, s * TB + i + 1)
                        o = ot[:].rearrange("r b v d (a e) -> r (b v) a d e", a=4)[:, 4 * i:4 * i + 4, :, :, s]
                        src = ops_t[i % 2][:].rearrange("r (k a d) -> r k a d", k=4, a=4)
                        for k in range(4):
                            last = nc.scalar.activation(o[:, k], src[:, k], ACT.Copy)
                        last.then_inc(back_used, 1)

                rolled(act, PARTS, part)
                act.wait_ge(roots_in, 2)
                nc.scalar.activation(root[:], v1[:], ACT.Sqrt).then_inc(roots, 1)

            @block.tensor
            def _(pe):
                agv = ag[:].rearrange("p b g s -> p (b g) s")
                nc.tensor.matmul(small[:, 0:BG], ones[:], agv[:, :, 0], start=True, stop=True).then_inc(sums, 1)
                pe.wait_ge(sums_in, 1)
                nc.tensor.matmul(small[:, 0:BG], ones[:], v1[:], start=True, stop=True).then_inc(sums, 1)
                pe.wait_ge(roots_in, 1)

                def part(s):
                    pe.wait_ge(sx_done, s + 1)
                    need(pe, xt_done, s)
                    alone(pe, passed)
                    for b in range(B):
                        last = nc.tensor.transpose(small[:, b * RI:(b + 1) * RI],
                                                   sx[:, b].rearrange("r a c -> r (a c)"), ident[0:RI, 0:RI])
                    last.then_inc(xt_ps, 1)
                    pe.wait_ge(xt_done, s + 1)
                    need(pe, os_done, s)
                    alone(pe, passed)
                    for turn in range(4):
                        for q in range(MODES // 4):
                            for a in range(4):
                                k = (turn + a) % 4
                                rows = slice(C * a, C * (a + 1))
                                last = nc.tensor.matmul(
                                    ops[rows, k, q * 32:(q + 1) * 32], wst[rows, k * (MODES // 4) + q],
                                    xt[rows, k * (MODES // 4) + q].rearrange("c b v -> c (b v)"),
                                    start=True, stop=True)
                    last.then_inc(mixed, 1)
                    pe.wait_ge(os_done, s + 1)
                    for i in range(TB):
                        need(pe, back_used, s * TB + i - 1)
                        alone(pe, passed)
                        for k in range(4):
                            b, v = 2 * i + k // 2, k % 2
                            last = nc.tensor.transpose(
                                ops_t[i % 2][:, k * P:(k + 1) * P],
                                os[:, 4 * b + 2 * v:4 * b + 2 * v + 2].rearrange("p r q -> p (r q)"), ident[:])
                        last.then_inc(back, 1)

                rolled(pe, PARTS, part)
                pe.wait_ge(sums_in, 2)
                nc.tensor.matmul(small[:, 0:BG], ws_t[:, 0], sxy[:], start=True, stop=False)
                nc.tensor.matmul(small[:, 0:BG], ws_t[:, 1], syy[:], start=False, stop=True).then_inc(sums, 1)
                nc.tensor.matmul(ops[:, 0, 0:BG], onerow[:], my[:], start=True, stop=True).then_inc(sums, 1)

            @block.sync
            def _(sp):
                sp.wait_ge(modes_out, 1)
                for b in range(B):
                    for twice in range(2):
                        sp.dma_start(od[b, :, twice], ot[:, b].rearrange("r v d p -> r (v d p)")).then_inc(stored, 16)
                sp.wait_ge(stored, 2 * 16 * B)


def gradient_pass(nc, sb, ps, sem, x, out, od, strip_y, ew_t, eh_hi, eh_lo, hmat, mean1, gscale,
                  strip_mean, strip_scale, eps_t):
    LAG_LO, LAG_GRAD, LAG_SQ, LAG_SUM, LAG_MAG, LAG_OUT = 1, 2, 3, 3, 4, 4
    UNROLL = 4
    PER = GROUPS // UNROLL
    with ExitStack() as gr:
        xb = sb("xb", [P, 2, WB, C], at=gr)
        g_t = sb("g_t", [P, 2, C, WB], F32R, at=gr)
        stage = sb("stage", [RI, UNROLL, 4, MODES], at=gr)
        x1 = sb("x1", [P, RING, GROUP, WB], at=gr)
        pr = sb("pr", [P, 2, GROUP, PAIRS + 1], at=gr)
        phi = sb("phi", [P, 2, GROUP, PAIRS + 1], F32R, at=gr)
        plo = sb("plo", [P, 2, GROUP, PAIRS + 1], F32R, at=gr)
        sq = sb("sq", [P, 2, 2, 512], at=gr)
        ssum = sb("ssum", [P, 2, 512], at=gr)
        mag = sb("mag", [P, 2, 512], at=gr)
        ghost = sb("ghost", [P, 4, C], at=gr)
        yps = ps("yps", [P, 2, 512], gr)
        gps = [ps(f"gps{i}", [P, 2, 512], gr) for i in range(2)]
        mps = ps("mps", [P, 512], gr)
        aside = sb("aside", [STRIP, UNROLL, WB], at=gr)

        x_in, ghosts, x_out = sem("x_in"), sem("ghosts"), sem("x_out")
        ghost_link = sem("ghost_link")
        y_done, x1_done, pairs_done = sem("y_done"), sem("x1_done"), sem("pairs_done")
        hi_done, lo_done, grad_done = sem("hi_done"), sem("lo_done"), sem("grad_done")
        sq_done, sum_done, mag_done, out_done = sem("sq_done"), sem("sum_done"), sem("mag_done"), sem("out_done")
        staged = [sem(f"staged{i}") for i in range(UNROLL)]
        g_ps, g_hi, g_lo = sem("g_ps"), sem("g_hi"), sem("g_lo")
        passed = sem("gradient_passed")
        strip_done, strip_copied = sem("strip_done"), sem("strip_copied")
        strip_out = [sem(f"strip_out{i}") for i in range(UNROLL)]
        strip_in = sem("strip_in")

        def steps(engine, n, emit):
            for k in range(BLOCKS if not isinstance(n, int) or n < TURNS else 2):
                if k == 0 and isinstance(n, int) and n == 0:
                    for g in range(GROUPS):
                        emit(k, g // UNROLL * UNROLL, g % UNROLL)
                    continue
                for j in range(UNROLL):
                    emit(k, 0, j)
                with engine.Fori(1, GROUPS // UNROLL) as i:
                    for j in range(UNROLL):
                        emit(k, i * UNROLL, j)

        def turns(engine, turn):
            turn(0)
            with engine.Fori(1, TURNS - 1) as n:
                turn(n)
            turn(TURNS - 1)
            turn(TURNS)

        class Step:

            def __init__(self, n, k, g0, j, lag=0):
                self.number = n * STEPS + k * GROUPS + g0 + (j - lag)
                if isinstance(g0, int) and g0 + j < lag:
                    k, g0 = k - 1, g0 + GROUPS
                    if k < 0:
                        k, n = BLOCKS - 1, n - 1
                self.strip = isinstance(n, int) and n == TURNS
                self.exists = not (isinstance(n, int) and n < 0) and not (self.strip and k == 2)
                self.turn, self.block, self.slot = n, k, k % 2
                self.g = g0 + (j - lag)
                self.ring = (g0 + (j - lag + RING)) % RING
                self.two = (j - lag) % 2
                self.variant = 2 if self.strip else VARIANT[k]

            def of_group(self, table, strip_table):
                if self.strip:
                    return strip_table[:, bass.ds(self.g, 1)]
                return table[:, bass.ds(self.turn % B * GROUPS + self.g, 1)]

        last_steps = [(2, 0, j) for j in range(LAG_OUT)]

        SPREAD, ASIDE = (1, 2), (0, 3)

        def spreads(n, k):
            return k in SPREAD and not (isinstance(n, int) and n >= TURNS - 1)

        def asides(n, k):
            return k in ASIDE and not (isinstance(n, int) and n >= TURNS)

        with nc.Block() as block:
            @block.sync
            def _(sp):
                def load(n, k):
                    half = n // B
                    src = x[n % B, ROW0[k]:ROW0[k] + P, bass.ds(half * (W - WIN), WIN), :]
                    sp.dma_start(xb[:, k % 2, bass.ds(half * -2 + 2, WIN), :], src).then_inc(x_in, 16)

                def load_strips(half):
                    w0, at = half * (W - WIN), 2 - 2 * half
                    for b in range(B):
                        sp.dma_start(xb[b * STRIP:(b + 1) * STRIP, half, at:at + WIN, :],
                                     x[b, STRIP0:, w0:w0 + WIN, :]).then_inc(x_in, 16)

                def load_strip_y(half):
                    sp.wait_ge(y_done, (TURNS - 1 + half) * STEPS)
                    sp.wait_ge(strip_done, (TURNS - 1 + half) * C)
                    for j in range(UNROLL):
                        sp.wait_ge(strip_out[j], 16 * (half + 1) * B * (C // UNROLL))
                    dst = g_t[:, half].rearrange("p c w -> p (c w)").bitcast(F32)
                    sp.dma_start(dst, strip_y[half].rearrange("b r c w -> (b r) (c w)")).then_inc(strip_in, 16)

                def store(n, k):
                    first, last = OUT[k]
                    cut = first + (last - first) // 16 * 16
                    for a, z in ((first, cut), (cut, last)):
                        r = a - ROW0[k]
                        sp.dma_start(out[n % B, a:z, bass.ds((n // B) * HALF, HALF), :],
                                     xb[r:r + z - a, k % 2, 2:2 + HALF, :]).then_inc(x_out, 16)

                def turn(n, last=False):
                    for k in range(BLOCKS):
                        sp.wait_ge(out_done, n * STEPS + (k + 1) * GROUPS)
                        store(n, k)
                        if last and k in (0, BLOCKS - 1):
                            if k > 0:
                                sp.wait_ge(strip_in, 16)
                            load_strip_y(1 if k else 0)
                        sp.wait_ge(x_out, 2 * 16 * (n * BLOCKS + k + 1))
                        sp.wait_ge(x_in, 16 * (n * BLOCKS + k + 2 + (B - 1) * (last and k == 3)))
                        if last and k >= 2:
                            load_strips(k - 2)
                        else:
                            load(n + (k + 2) // BLOCKS, (k + 2) % BLOCKS)

                load(0, 0)
                sp.wait_ge(x_in, 16)
                load(0, 1)
                with sp.Fori(0, TURNS - 1) as n:
                    turn(n)
                turn(TURNS - 1, last=True)
                for half in range(2):
                    sp.wait_ge(out_done, TURNS * STEPS + (half + 1) * GROUPS)
                    for b in range(B):
                        r = b * STRIP + OUT[-1][1] - STRIP0
                        sp.dma_start(out[b, OUT[-1][1]:, half * HALF:(half + 1) * HALF, :],
                                     xb[r:(b + 1) * STRIP, half, 2:2 + HALF, :]).then_inc(x_out, 16)
                sp.wait_ge(x_out, 2 * 16 * TURNS * BLOCKS + 2 * 16 * B)

            @block.gpsimd
            def _(pool):
                G = nc.gpsimd
                def fetch(m, i, slot):
                    need(pool, g_ps, (m * (C // UNROLL) + i - 1) * UNROLL + slot + 1)
                    src = od[m % B].rearrange("r t (v d p) -> r (t v) d p", v=2, d=C)[:, :, bass.ds(i * UNROLL + slot, 1), :]
                    pool.dma_start(stage[:, slot], src.rearrange("r v d p -> r v (d p)")).then_inc(staged[slot], 16)

                def ghosts_of(n, k):
                    slot, half, unit = k % 2, (k if isinstance(n, int) and n == TURNS else n // B), n * BLOCKS + k
                    loads = 16 * (unit + 1)
                    if isinstance(n, int) and n == TURNS:
                        loads = 16 * (TURNS * BLOCKS + (k + 1) * B)
                    pool.wait_ge(x_in, loads)

                    def col(left, right):
                        return xb[:, slot, bass.ds(half * (right - left) + left, 1), :].rearrange("p w c -> p (w c)")
                    edge, inner = col(2, WIN - 1), col(3, WIN - 2)
                    near, far = col(1, WIN), col(0, WIN + 1)

                    def then(step, ins):
                        ins.then_inc(ghost_link, 1)
                        pool.wait_ge(ghost_link, 4 * unit + step + 1)
                        alone(pool, passed)

                    alone(pool, passed)
                    then(0, G.tensor_tensor(ghost[:, 0], edge, inner, ALU.add))
                    then(1, G.tensor_scalar(ghost[:, 1], ghost[:, 0], 0.5, None, ALU.mult))
                    G.tensor_copy(near, ghost[:, 1])
                    then(2, G.tensor_tensor(ghost[:, 2], edge, ghost[:, 1], ALU.add))
                    then(3, G.tensor_scalar(ghost[:, 3], ghost[:, 2], -1.0, None, ALU.mult))
                    G.tensor_copy(far, ghost[:, 3]).then_inc(ghosts, 1)

                def fetches(m, first, count):
                    with pool.Fori(first, first + count) as i:
                        for slot in range(UNROLL):
                            fetch(m, i, slot)

                for slot in range(UNROLL):
                    fetch(0, 0, slot)
                fetches(0, 1, C // UNROLL - 1)
                ghosts_of(0, 0)

                def put_aside(n, i, slot):
                    pool.wait_ge(strip_copied, (n * (C // UNROLL) + i) * UNROLL + slot + 1)
                    dst = strip_y[n // B, n % B, :, bass.ds(i * UNROLL + slot, 1), :].rearrange("r c w -> r (c w)")
                    pool.dma_start(dst, aside[:, slot]).then_inc(strip_out[slot], 16)

                def asides_out(n, first, count):
                    with pool.Fori(first, first + count) as i:
                        for slot in range(UNROLL):
                            put_aside(n, i, slot)

                def turn(n):
                    if isinstance(n, int) and n == TURNS:
                        ghosts_of(TURNS, 1)
                        return
                    for k in range(BLOCKS):
                        first = PER * (k // 2)
                        if asides(n, k):
                            asides_out(n, first, PER - 1)
                        if spreads(n, k):
                            fetches(n + 1, (k - 1) * PER, PER)
                        ghosts_of(n + (k + 1) // BLOCKS, (k + 1) % BLOCKS)
                        if asides(n, k):
                            asides_out(n, first + PER - 1, 1)

                turns(pool, turn)

            @block.tensor
            def _(pe):
                T = nc.tensor

                def spread(m, i, slot):
                    pe.wait_ge(staged[slot], 16 * (m * (C // UNROLL) + i + 1))
                    need(pe, g_lo, (m * (C // UNROLL) + i) * UNROLL + slot)
                    if not (isinstance(m, int) and m == 0):
                        pe.wait_ge(strip_copied, m * C - C // 2)
                    alone(pe, passed)
                    modes = stage[:, slot].rearrange("r v p -> r (v p)")
                    half = ew_t[:, bass.ds(m // B % 2, 1), :].rearrange("r h w -> r (h w)")
                    T.matmul(mps[:, 0:WB], modes, half, start=True, stop=True).then_inc(g_ps, 1)

                def inverse_h(dst, s_turn, c, cols):
                    rhs = g_t[:, s_turn % 2, bass.ds(c, 1), :].rearrange("p c w -> p (c w)")
                    T.matmul(dst, eh_lo[:, cols], rhs, start=True, stop=False)
                    return T.matmul(dst, eh_hi[:, cols], rhs, start=False, stop=True)

                def put_aside(n, k, i, slot):
                    need(pe, strip_copied, (n * (C // UNROLL) + i) * UNROLL + slot)
                    pe.wait_ge(g_lo, (n + 1 + (k == BLOCKS - 1 and spreads(n, SPREAD[0]))) * C)
                    alone(pe, passed)
                    cols = slice(BLOCKS * P, BLOCKS * P + STRIP)
                    inverse_h(mps[0:STRIP, 0:WB], n, i * UNROLL + slot, cols).then_inc(strip_done, 1)

                def y(s):
                    need(pe, x1_done, s.number)
                    alone(pe, passed)
                    for ch in range(GROUP):
                        last = inverse_h(yps[:, ch, 0:WB], s.turn, s.g * GROUP + ch,
                                         slice(s.block * P, (s.block + 1) * P))
                    last.then_inc(y_done, 1)

                def grad(s):
                    if not s.exists:
                        return
                    pe.wait_ge(lo_done, s.number + 1)
                    need(pe, sq_done, s.number - 1)
                    taps = [[(0, 0), (1, 3)], [(2, 0), (3, 1), (3, 2), (2, 3)]]
                    for d in range(2):
                        todo = [(m, w, part) for m, w in taps[d] for part in (plo, phi)]
                        for i, (m, w, part) in enumerate(todo):
                            last = T.matmul(gps[s.two][:, d], hmat[:, s.variant, m],
                                            part[:, s.two, :, w:w + HALF],
                                            start=(i == 0), stop=(i == len(todo) - 1))
                    last.then_inc(grad_done, 1)

                for slot in range(UNROLL):
                    spread(0, 0, slot)
                with pe.Fori(1, C // UNROLL) as i:
                    for slot in range(UNROLL):
                        spread(0, i, slot)

                def turn(n):
                    def emit(k, g0, j):
                        s = Step(n, k, g0, j)
                        if not s.strip:
                            if k == 0 and isinstance(g0, int) and g0 + j == 0:
                                pe.wait_ge(g_lo, (n + 1) * C)
                            y(s)
                        grad(Step(n, k, g0, j, LAG_GRAD))
                        i = g0 // UNROLL
                        if spreads(n, k):
                            spread(n + 1, (k - 1) * PER + i, j)
                        if asides(n, k):
                            put_aside(n, k, (k // 2) * PER + i, j)
                    steps(pe, n, emit)

                turns(pe, turn)
                for k, g0, j in last_steps[:LAG_GRAD]:
                    grad(Step(TURNS, k, g0, j, LAG_GRAD))

            @block.scalar
            def _(act):
                A = nc.scalar

                def high(m, c):
                    act.wait_ge(g_ps, m * C + c + 1)
                    alone(act, passed)
                    dst = g_t[:, m % 2, bass.ds(c, 1), :].rearrange("p c w -> p (c w)")
                    A.activation(dst, mps[:, 0:WB], ACT.Copy).then_inc(g_hi, 1)

                def put_aside(n, c, i, slot):
                    act.wait_ge(strip_done, n * C + c + 1)
                    need(act, strip_out[slot], 16 * (n * (C // UNROLL) + i))
                    A.activation(aside[:, slot], mps[0:STRIP, 0:WB], ACT.Copy).then_inc(strip_copied, 1)

                def magnitude(s):
                    if not s.exists:
                        return
                    act.wait_ge(sum_done, s.number + 1)
                    need(act, out_done, s.number - 1)
                    alone(act, passed)
                    scale = s.of_group(gscale, strip_scale)
                    A.activation(mag[:, s.two], ssum[:, s.two], ACT.Sqrt, bias=eps_t[:], scale=scale).then_inc(mag_done, 1)

                def squares(s):
                    if not s.exists:
                        return
                    act.wait_ge(grad_done, s.number + 1)
                    need(act, sum_done, s.number - 1)
                    A.activation(sq[:, s.two], gps[s.two][:], ACT.Square).then_inc(sq_done, 1)

                def high_pairs(s):
                    act.wait_ge(pairs_done, s.number + 1)
                    need(act, grad_done, s.number - 1)
                    A.activation(phi[:, s.two, :, 0:PAIRS], pr[:, s.two, :, 0:PAIRS], ACT.Copy).then_inc(hi_done, 1)

                with act.Fori(0, C) as c:
                    high(0, c)

                def turn(n):
                    def emit(k, g0, j):
                        magnitude(Step(n, k, g0, j, LAG_MAG))
                        squares(Step(n, k, g0, j, LAG_SQ))
                        high_pairs(Step(n, k, g0, j))
                        if spreads(n, k):
                            high(n + 1, (k - 1) * GROUPS + g0 + j)
                        if asides(n, k):
                            put_aside(n, (k // 2) * GROUPS + g0 + j, (k // 2) * PER + g0 // UNROLL, j)
                    steps(act, n, emit)

                turns(act, turn)
                for k, g0, j in last_steps:
                    magnitude(Step(TURNS, k, g0, j, LAG_MAG))
                    if j < LAG_SQ:
                        squares(Step(TURNS, k, g0, j, LAG_SQ))

            @block.vector
            def _(dve):
                V = nc.vector

                def low(m, c):
                    dve.wait_ge(g_hi, m * C + c + 1)
                    dst = g_t[RI:P, m % 2, bass.ds(c, 1), :].rearrange("p c w -> p (c w)")
                    V.tensor_tensor(dst, mps[RI:P, 0:WB], dst.bitcast(F32), ALU.subtract).then_inc(g_lo, 1)

                def add_y(s):
                    if s.strip:
                        y = g_t[:, s.block, bass.ds(s.g * GROUP, GROUP)].bitcast(F32)
                    else:
                        dve.wait_ge(y_done, s.number + 1)
                        y = yps[:, :, 0:WB]
                    src = xb[:, s.slot, :, bass.ds(s.g * GROUP, GROUP)].rearrange("p w c -> p c w")
                    V.tensor_tensor(x1[:, s.ring], src, y, ALU.add).then_inc(x1_done, 1)

                def low_pairs(s):
                    if not s.exists:
                        return
                    dve.wait_ge(hi_done, s.number + 1)
                    need(dve, grad_done, s.number - 1)
                    V.tensor_tensor(plo[:, s.two, :, 0:PAIRS], pr[:, s.two, :, 0:PAIRS],
                                    phi[:, s.two, :, 0:PAIRS].bitcast(F32), ALU.subtract).then_inc(lo_done, 1)

                def pairs(s):
                    dve.wait_ge(x1_done, s.number + 1)
                    V.tensor_tensor(pr[:, s.two, :, 0:PAIRS], x1[:, s.ring, :, 0:PAIRS],
                                    x1[:, s.ring, :, 1:WB], ALU.add).then_inc(pairs_done, 1)

                def add_squares(s):
                    if not s.exists:
                        return
                    dve.wait_ge(sq_done, s.number + 1)
                    need(dve, mag_done, s.number - 1)
                    V.tensor_tensor(ssum[:, s.two], sq[:, s.two, 0], sq[:, s.two, 1], ALU.add).then_inc(sum_done, 1)

                def result(s):
                    if not s.exists:
                        return
                    dve.wait_ge(mag_done, s.number + 1)
                    dst = xb[:, s.slot, 2:2 + HALF, bass.ds(s.g * GROUP, GROUP)].rearrange("p w c -> p c w")
                    V.scalar_tensor_tensor(dst, x1[:, s.ring, :, 2:2 + HALF],
                                           s.of_group(mean1, strip_mean),
                                           mag[:, s.two].rearrange("p (c w) -> p c w", c=GROUP),
                                           ALU.add, ALU.add).then_inc(out_done, 1)

                with dve.Fori(0, C) as c:
                    low(0, c)

                def turn(n):
                    def emit(k, g0, j):
                        if isinstance(g0, int) and g0 + j == 0:
                            dve.wait_ge(ghosts, n * BLOCKS + k + 1)
                            if isinstance(n, int) and n == TURNS:
                                dve.wait_ge(strip_in, 16 * (k + 1))
                        add_y(Step(n, k, g0, j))
                        low_pairs(Step(n, k, g0, j, LAG_LO))
                        pairs(Step(n, k, g0, j))
                        add_squares(Step(n, k, g0, j, LAG_SUM))
                        result(Step(n, k, g0, j, LAG_OUT))
                        if spreads(n, k):
                            low(n + 1, (k - 1) * GROUPS + g0 + j)
                    steps(dve, n, emit)

                turns(dve, turn)
                for k, g0, j in last_steps:
                    if j < LAG_LO:
                        low_pairs(Step(TURNS, k, g0, j, LAG_LO))
                    if j < LAG_SUM:
                        add_squares(Step(TURNS, k, g0, j, LAG_SUM))
                    result(Step(TURNS, k, g0, j, LAG_OUT))


def kernel(x, L0_conv_W):
    import concourse.bacc as bacc
    from concourse.bass_utils import run_bass_kernel_spmd

    nc = bacc.Bacc("TRN2", target_bir_lowering=False, num_devices=1)
    tab = tables()
    arrays = {"x_dram": np.ascontiguousarray(x), "w_dram": np.ascontiguousarray(L0_conv_W)}
    arrays.update({f"{n}_dram": a for n, a in tab.items()})
    aps = {n: nc.dram_tensor(n, a.shape, mybir.dt.from_np(a.dtype), kind="ExternalInput").ap()
           for n, a in arrays.items()}
    out = nc.dram_tensor("out_dram", (B, H, W, C), F32, kind="ExternalOutput").ap()
    od = nc.dram_tensor("mixed_modes", (B, RI, 2, 2 * C * MODES), F32, kind="Internal").ap()
    strip_y = nc.dram_tensor("strip_y", (2, B, STRIP, C, WB), F32, kind="Internal").ap()
    spectral_gradient_kernel(nc, aps["x_dram"], aps["w_dram"], {n: aps[f"{n}_dram"] for n in tab}, out, od, strip_y)
    r = run_bass_kernel_spmd(nc, [arrays], core_ids=[0])
    return r.results[0]["out_dram"]
```

```python
from contextlib import ExitStack

import numpy as np

import concourse.bass as bass
from concourse import mybir

F32 = mybir.dt.float32
F32R = mybir.dt.float32r
ALU = mybir.AluOpType
ACT = mybir.ActivationFunctionType
AX = mybir.AxisListType

B, H, W, C = 8, 512, 512, 32
N = 512
MODES = 32
GROUP = 2
GROUPS = C // GROUP
BG = B * GROUPS
P = 128
RI = 2 * MODES
EPS_GN = 1e-5
EPS_GRAD = 1e-6

HALF = W // 2
WIN = HALF + 2
WB = WIN + 2
PAIRS = WB - 1
ROW0 = [0, 124, 248, 372]
OUT = [(0, 126), (126, 250), (250, 374), (374, 498)]
BLOCKS = len(ROW0)
STRIP = P // B
STRIP0 = H - STRIP
VARIANT = [0, 1, 1, 1]
TURNS = 2 * B
STEPS = BLOCKS * GROUPS
RING = 8

CW = 32
CHUNKS = W // CW
HB = H // P
XRING = 4
WBLK = W // P
PER_BLK = P // CW
SUB = 512 // C


def tables():
    k = np.arange(MODES)
    ang = 2 * np.pi * np.outer(np.arange(N), k) / N
    cos, sin = np.cos(ang), np.sin(ang)
    fh = np.concatenate([cos, -sin], 1).reshape(HB, P, RI).transpose(1, 0, 2)
    fw = np.stack([np.concatenate([cos, -sin], 1), np.concatenate([sin, cos], 1)], 1)
    fw = fw.reshape(WBLK, P, 2, RI).transpose(1, 0, 2, 3)
    alpha = np.where(k == 0, 1.0, 2.0)
    rows = np.concatenate([cos * alpha, sin * alpha], 1).T / N
    left = np.concatenate([-(1.5 * rows[:, :1] + 0.5 * rows[:, 1:2]), 0.5 * (rows[:, :1] + rows[:, 1:2]),
                           rows[:, :WIN]], 1)
    right = np.concatenate([rows[:, W - WIN:], 0.5 * (rows[:, -1:] + rows[:, -2:-1]),
                            -(1.5 * rows[:, -1:] + 0.5 * rows[:, -2:-1])], 1)
    ew = np.stack([left, right], 1)
    ew = np.tile(ew, (2, 1, 1))
    both = np.tile(np.concatenate([cos, -sin], 1).T / N, (2, 1))
    eh = np.concatenate([both[:, r0:r0 + P] for r0 in ROW0] + [both[:, STRIP0:]], 1)
    pool = sum(np.eye(H, k=d) for d in (-1, 0, 1))
    pool[0] *= 1.5
    pool[-1] *= 1.5
    smooth = (2 * np.eye(H) + np.eye(H, k=1) + np.eye(H, k=-1)) @ pool
    diff = (np.eye(H, k=-1) - np.eye(H, k=1)) @ pool
    hm = np.zeros((P, 3, 2, P))
    for i, m in enumerate((smooth, diff)):
        for v, r0 in enumerate(ROW0[:2]):
            hm[:, v, i] = m[r0:r0 + P, r0:r0 + P].T
        hm[:, 2, i] = np.kron(np.eye(B), m[STRIP0:, STRIP0:].T)
    sign = np.concatenate([alpha, -alpha])
    beta = np.where(k == 0, 0.5, 2.0)
    ws = np.stack([2 * sign, np.concatenate([beta, beta])], 1) / N**2 / (GROUP * H * W)
    ws = np.repeat(ws[:, :, None], P, 2)
    t = {"fh": fh, "fw": fw, "ew": ew, "eh": eh, "hm": hm, "ws": ws, "ones": np.full((P, P), 1 / P),
         "onerow": np.full((1, P), 1 / (GROUP * N**2)), "ident": np.eye(P), "owner": np.kron(np.eye(B), np.ones((STRIP, 1)))}
    return {n: np.ascontiguousarray(a, np.float32) for n, a in t.items()}


def spectral_gradient_kernel(nc, x, w_modes, tab, out, od, strip_y):
    ctx = ExitStack()
    with ctx:
        def sb(name, shape, dt=F32, at=ctx):
            return at.enter_context(nc.sbuf_tensor(name, shape, dt))

        def ps(name, shape, at):
            return at.enter_context(nc.psum_tensor(name, shape, F32))

        def sem(name):
            return ctx.enter_context(nc.semaphore(name))

        ew_hi = sb("ew_hi", [P, 2, WB], F32R)
        ew_lo = sb("ew_lo", [P, 2, WB], F32R)
        eh_hi = sb("eh_hi", [P, BLOCKS * P + STRIP], F32R)
        eh_lo = sb("eh_lo", [P, BLOCKS * P + STRIP], F32R)
        hmat = sb("hmat", [P, 3, 4, P], F32R)
        mean1 = sb("mean1", [P, BG])
        gscale = sb("gscale", [P, BG])
        strip_mean = sb("strip_mean", [P, GROUPS])
        strip_scale = sb("strip_scale", [P, GROUPS])
        eps_t = sb("eps_t", [P, 1])

        spectra = ExitStack()
        with spectra:
            fh_t = sb("fh_t", [P, HB, RI], at=spectra)
            fw_t = sb("fw_t", [P, WBLK, 2, RI], at=spectra)
            ident = sb("ident_t", [P, P], at=spectra)
            ones = sb("ones_t", [P, P], at=spectra)
            onerow = sb("onerow_t", [1, P], at=spectra)
            owner = sb("owner_t", [P, B], at=spectra)
            ws_t = sb("ws_t", [RI, 2, P], at=spectra)
            wt = sb("wt", [P, MODES // 4, MODES, C], at=spectra)
            xs = sb("xs", [RI, B, C, MODES], at=spectra)
            ag = sb("ag", [P, B, GROUPS, 2], at=spectra)
            forward_pass(nc, sb, ps, sem, x, w_modes, tab, fh_t, fw_t, ident, ones, onerow, owner, ws_t, wt, xs, ag, eps_t)
            modes_pass(nc, sb, ps, sem, od, tab, ident, ones, onerow, owner, ws_t, wt, xs, ag, ew_hi, ew_lo,
                       eh_hi, eh_lo, hmat, mean1, gscale, strip_mean, strip_scale)
        gradient_pass(nc, sb, ps, sem, x, out, od, strip_y, ew_hi, ew_lo, eh_hi, eh_lo, hmat, mean1, gscale,
                      strip_mean, strip_scale, eps_t)


def need(engine, semaphore, count):
    if not (isinstance(count, int) and count <= 0):
        engine.wait_ge(semaphore, count)


def alone(engine, passed):
    engine.sem_inc(passed, 1)


def rolled(engine, count, body):
    body(0)
    with engine.Fori(1, count) as i:
        body(i)


def forward_pass(nc, sb, ps, sem, x, w_modes, tab, fh_t, fw_t, ident, ones, onerow, owner, ws_t, wt, xs, ag, eps_t):
    with ExitStack() as fwd:
        xa = sb("xa", [P, XRING, HB, CW * C], at=fwd)
        zs = sb("zs", [RI, 2, P, C], at=fwd)
        zt = sb("zt", [P, C, RI], at=fwd)
        bn = sb("bn", [P, GROUPS, CHUNKS, 6], at=fwd)
        merged = sb("merged", [P, GROUPS, 2], at=fwd)
        zps = [ps(f"zps{i}", [RI, 512], fwd) for i in range(2)]
        tps = [ps(f"tps{i}", [P, 512], fwd) for i in range(2)]
        xps = ps("xps", [RI, C * MODES], fwd)

        loaded = [sem(f"chunk_loaded{i}") for i in range(XRING)]
        tables_in, weights_in = sem("tables_in"), sem("weights_in")
        chunk_counted = sem("chunk_counted")
        z_done, z_used = sem("z_done"), sem("z_used")
        t_done, t_used = sem("t_done"), sem("t_used")
        modes_done, modes_used = sem("modes_done"), sem("modes_used")
        image_merged, passed = sem("image_merged"), sem("forward_passed")

        loads = [(fh_t, "fh"), (fw_t, "fw"), (ident, "ident"), (ones, "ones"), (onerow, "onerow"), (owner, "owner"),
                 (ws_t, "ws")]
        x_v = x.rearrange("b (t p) w c -> b p t (w c)", p=P)
        w_v = w_modes.rearrange("(r s) q c d -> r c s q d", r=4)
        CH = 512 // RI
        ZB = CW // SUB

        with nc.Block() as block:
            @block.sync
            def _(sp):
                for t, name in loads:
                    sp.dma_start(t[:], tab[name]).then_inc(tables_in, 16)

                def ring(i):
                    for j in range(XRING):
                        need(sp, z_done, ((i - 1) * XRING + j + 1) * ZB)
                        need(sp, chunk_counted, (i - 1) * XRING + j + 1)
                        at = (i * XRING + j) % CHUNKS * (CW * C)
                        sp.dma_start(xa[:, j], x_v[i * XRING // CHUNKS, :, :, bass.ds(at, CW * C)]
                                     ).then_inc(loaded[j], 16)

                rolled(sp, B * CHUNKS // XRING, ring)

            @block.gpsimd
            def _(pool):
                nc.gpsimd.memset(eps_t[:], EPS_GRAD)
                for r in range(4):
                    for s in range(MODES // 4):
                        pool.dma_start(wt[r * C:(r + 1) * C, s], w_v[r, :, s]).then_inc(weights_in, 16)
                pool.wait_ge(weights_in, 16 * MODES)

            @block.tensor
            def _(pe):
                pe.wait_ge(tables_in, 16 * len(loads))

                def image(b):
                    for k in range(WBLK):
                        blk = b * WBLK + k
                        for j in range(PER_BLK):
                            chunk = blk * PER_BLK + j
                            pe.wait_ge(loaded[j], 16 * (blk + 1))
                            for s in range(ZB):
                                need(pe, z_used, (chunk - 1) * ZB + s + 1)
                                for t in range(HB):
                                    last = nc.tensor.matmul(
                                        zps[s][:], fh_t[:, t], xa[:, j, t, s * 512:(s + 1) * 512],
                                        start=(t == 0), stop=(t == HB - 1))
                                last.then_inc(z_done, 1)
                        pe.wait_ge(z_used, (blk + 1) * PER_BLK * ZB)
                        for o in range(C // CH):
                            need(pe, t_used, blk * (C // CH) + o - 1)
                            alone(pe, passed)
                            for c in range(CH):
                                last = nc.tensor.transpose(tps[o % 2][:, c * RI:(c + 1) * RI],
                                                           zs[:, k % 2, :, o * CH + c], ident[0:RI, 0:RI])
                            last.then_inc(t_done, 1)
                        if k == 0:
                            need(pe, modes_used, b)
                        for half in range(2):
                            pe.wait_ge(t_used, blk * (C // CH) + 2 * half + 2)
                            for part in range(2):
                                last = nc.tensor.matmul(
                                    xps[:, half * 512:(half + 1) * 512], fw_t[:, k, part],
                                    zt[:, half * 16:(half + 1) * 16, part * MODES:(part + 1) * MODES],
                                    start=(k == 0 and part == 0), stop=(k == WBLK - 1 and part == 1))
                        last.then_inc(modes_done, 1)

                rolled(pe, B, image)

            @block.scalar
            def _(act):
                def image(b):
                    for k in range(WBLK):
                        blk = b * WBLK + k
                        for z in range(PER_BLK * ZB):
                            act.wait_ge(z_done, blk * PER_BLK * ZB + z + 1)
                            need(act, modes_done, blk - 1)
                            nc.scalar.activation(zs[:, k % 2, z * SUB:(z + 1) * SUB], zps[z % ZB][:],
                                                 ACT.Copy).then_inc(z_used, 1)
                        for o in range(C // CH):
                            act.wait_ge(t_done, blk * (C // CH) + o + 1)
                            need(act, modes_done, blk)
                            nc.scalar.activation(zt[:, o * CH:(o + 1) * CH], tps[o % 2][:],
                                                 ACT.Copy).then_inc(t_used, 1)
                    act.wait_ge(modes_done, (b + 1) * WBLK)
                    alone(act, passed)
                    nc.scalar.activation(xs[:, b], xps[:], ACT.Copy).then_inc(modes_used, 1)

                rolled(act, B, image)

            @block.vector
            def _(dve):
                def image(b):
                    for i in range(CHUNKS):
                        dve.wait_ge(loaded[i % XRING], 16 * (b * (CHUNKS // XRING) + i // XRING + 1))
                        if i == 0:
                            need(dve, image_merged, b)
                        v = xa[:, i % XRING].rearrange("p t (w c) -> p t w c", c=C)
                        for g in range(GROUPS):
                            last = nc.vector.bn_stats(bn[:, g, i], v[:, :, :, GROUP * g:GROUP * (g + 1)])
                        last.then_inc(chunk_counted, 1)
                    dve.wait_ge(chunk_counted, (b + 1) * CHUNKS)
                    alone(dve, passed)
                    for g in range(GROUPS):
                        last = nc.vector.bn_aggr(merged[:, g], bn[:, g])
                    last.then_inc(image_merged, 1)
                    dve.wait_ge(image_merged, b + 1)
                    nc.vector.tensor_copy(ag[:, b], merged[:])

                rolled(dve, B, image)


def modes_pass(nc, sb, ps, sem, od, tab, ident, ones, onerow, owner, ws_t, wt, xs, ag, ew_hi, ew_lo,
               eh_hi, eh_lo, hmat, mean1, gscale, strip_mean, strip_scale):
    with ExitStack() as mod:
        split = sb("split", [P, B, C, 2, MODES], F32R, at=mod)
        mx = sb("mx", [RI, B, 2, 4, C], at=mod)
        prod = sb("prod", [RI, 2, B, C, 4], at=mod)
        part_sum = sb("part_sum", [RI, 2, BG], at=mod)
        sxy = sb("sxy", [RI, 2, BG], at=mod)
        dc = sb("dc", [1, B, C], at=mod)
        dc_parts = sb("dc_parts", [1, 2, B, C], F32R, at=mod)
        r0c = sb("r0c", [RI, B, C], at=mod)
        sx = sb("sx", [RI, B, 4, C], at=mod)
        xt = sb("xt", [P, MODES, B, 4], at=mod)
        wst = sb("wst", [P, MODES, C], at=mod)
        os = sb("os", [P, B * 4, MODES], at=mod)
        m0 = sb("m0", [P, BG], at=mod)
        v0 = sb("v0", [P, BG], at=mod)
        v1 = sb("v1", [P, BG], at=mod)
        root = sb("root", [P, BG], at=mod)
        inv = sb("inv", [P, BG], at=mod)
        r0 = sb("r0", [P, BG], at=mod)
        tmp = sb("tmp", [P, BG], at=mod)
        my = sb("my", [1, BG], at=mod)
        ew_raw = sb("ew_raw", [P, 2, WB], at=mod)
        eh_raw = sb("eh_raw", [P, BLOCKS * P + STRIP], at=mod)
        hm_raw = sb("hm_raw", [P, 3, 2, P], at=mod)
        small = ps("small", [P, 512], mod)
        ops = ps("ops", [P, 4, 512], mod)
        ops_t = [ps(f"ops_t{i}", [RI, 512], mod) for i in range(2)]

        link, part_link = sem("dve_link"), sem("part_link")
        sums_in, sums = sem("sums_in"), sem("sums")
        roots_in, roots = sem("roots_in"), sem("roots")
        raw_in, tables_hi = sem("raw_in"), sem("tables_hi")
        sx_done, wst_done, xt_ps, xt_done = sem("sx_done"), sem("wst_done"), sem("xt_ps"), sem("xt_done")
        mixed, os_done = sem("mixed"), sem("os_done")
        back, back_used = sem("back"), sem("back_used")
        modes_hi, modes_lo, mx_used = sem("modes_hi"), sem("modes_lo"), sem("mx_used")
        patched, stored = sem("modes_patched"), sem("modes_stored")
        passed = sem("modes_passed")

        TB = 4
        PARTS = MODES // 4

        def parts(engine, part):
            part(0)
            with engine.Fori(1, PARTS - 1) as s:
                part(s)
            part(PARTS - 1, last=True)

        def of_part(t, s):
            return t.rearrange("r b c (a e) -> r b a c e", a=4)[:, :, :, :, s]

        with nc.Block() as block:
            @block.vector
            def _(dve):
                V = nc.vector
                count = [0]

                def then(ins):
                    count[0] += 1
                    ins.then_inc(link, 1)
                    dve.wait_ge(link, count[0])

                def inverse_root(out, var, step):
                    dve.wait_ge(roots, step)
                    then(V.reciprocal(inv[:], root[:]))
                    then(V.tensor_tensor(tmp[:], inv[:], inv[:], ALU.mult))
                    then(V.tensor_tensor(tmp[:], tmp[:], var[:], ALU.mult))
                    then(V.tensor_scalar(tmp[:], tmp[:], -0.5, 1.5, ALU.mult, ALU.add))
                    then(V.tensor_tensor(out[:], inv[:], tmp[:], ALU.mult))

                V.tensor_copy(wst[:], wt[:, 0]).then_inc(wst_done, 1)
                dve.wait_ge(sums, 1)
                then(V.tensor_copy(m0[:], small[:, 0:BG]))
                agv = ag[:].rearrange("p b g s -> p (b g) s")
                then(V.tensor_tensor(tmp[:], agv[:, :, 0], m0[:], ALU.subtract))
                then(V.tensor_tensor(tmp[:], tmp[:], tmp[:], ALU.mult))
                V.tensor_tensor(v1[:], tmp[:], agv[:, :, 1], ALU.add).then_inc(sums_in, 1)
                dve.wait_ge(sums, 2)
                V.tensor_scalar(v0[:], small[:, 0:BG], EPS_GN, None, ALU.add).then_inc(roots_in, 1)
                inverse_root(r0, v0, 1)
                x0 = xs[0:1].rearrange("r b (g s) p -> r (b g) s p", s=GROUP)[:, :, :, 0]
                V.scalar_tensor_tensor(x0, m0[0:1, :, None].to_broadcast([1, BG, GROUP]), -float(H * W), x0,
                                       ALU.mult, ALU.add)
                then(V.tensor_copy(r0c[:].rearrange("r b (g s) -> r (b g) s", s=GROUP),
                                   r0[0:RI, :, None].to_broadcast([RI, BG, GROUP])))

                def scaled(s):
                    V.tensor_tensor(sx[:], of_part(xs[:], s), r0c[:, :, None, :].to_broadcast([RI, B, 4, C]),
                                    ALU.mult).then_inc(sx_done, 1)

                scaled(0)
                dve.wait_ge(tables_hi, 1)
                V.tensor_tensor(eh_lo[:], eh_raw[:], eh_hi[:].bitcast(F32), ALU.subtract)
                V.tensor_tensor(ew_lo[:], ew_raw[:], ew_hi[:].bitcast(F32), ALU.subtract)

                def part(s, last=False):
                    if not last:
                        dve.wait_ge(xt_ps, s + 1)
                        scaled(s + 1)
                        dve.wait_ge(mixed, s + 1)
                        alone(dve, passed)
                        V.tensor_copy(wst[:], wt[:, s + 1]).then_inc(wst_done, 1)
                    for v in range(2):
                        dve.wait_ge(modes_hi, 2 * s + v + 1)
                        alone(dve, passed)
                        ins = V.tensor_tensor(of_part(split[RI:P, :, :, v], s), mx[:, :, v],
                                              of_part(split[0:RI, :, :, v], s).bitcast(F32), ALU.subtract)
                    ins.then_inc(modes_lo, 1)

                    def then_part(step, ins):
                        ins.then_inc(part_link, 1)
                        dve.wait_ge(part_link, s * 2 + step)

                    y = mx[:, :, 0]
                    V.tensor_tensor(prod[:, 0].rearrange("r b c a -> r b a c"), y, of_part(xs[:], s), ALU.mult)
                    then_part(1, V.tensor_tensor(prod[:, 1].rearrange("r b c a -> r b a c"), y, y, ALU.mult))
                    if isinstance(s, int) and s == 0:
                        V.tensor_copy(dc[:], mx[0:1, :, 0, 0, :])
                        for row in (0, MODES):
                            for i in range(2):
                                ins = V.memset(prod[row:row + 1, i, :, :, 0], 0.0)
                        then(ins)
                    sums_of = prod[:].rearrange("r i b (g s) a -> r (i b g) (s a)", s=GROUP)
                    dst = sxy if isinstance(s, int) and s == 0 else part_sum
                    then_part(2, V.tensor_reduce(dst[:].rearrange("r i g -> r (i g)"), sums_of, axis=AX.X, op=ALU.add))
                    if dst is part_sum:
                        V.tensor_tensor(sxy[:], sxy[:], part_sum[:], ALU.add).then_inc(mx_used, 1)
                    else:
                        dve.sem_inc(mx_used, 1)
                    dve.wait_ge(mx_used, s + 1)

                parts(dve, part)

                V.tensor_reduce(my[:], dc[:].rearrange("r b (g s) -> r (b g) s", s=GROUP), axis=AX.X, op=ALU.add
                                ).then_inc(sums_in, 1)
                dve.wait_ge(sums, 4)
                then(V.tensor_tensor(tmp[:], v0[:], small[:, 0:BG], ALU.add))
                V.tensor_scalar(v1[:], tmp[:], EPS_GN, None, ALU.max).then_inc(roots_in, 1)
                then(V.tensor_tensor(mean1[:], m0[:], ops[:, 0, 0:BG], ALU.add))
                dcv = dc[:].rearrange("r b (g s) -> r (b g) s", s=GROUP)
                then(V.scalar_tensor_tensor(dcv, mean1[0:1, :, None].to_broadcast([1, BG, GROUP]), -float(H * W), dcv,
                                            ALU.mult, ALU.add))
                then(V.tensor_copy(dc_parts[:, 0], dc[:]))
                V.tensor_tensor(dc_parts[:, 1], dc[:], dc_parts[:, 0].bitcast(F32), ALU.subtract).then_inc(patched, 1)
                inverse_root(r0, v1, 2)
                then(V.tensor_tensor(tmp[:], r0[:], r0[:], ALU.mult))
                then(V.tensor_scalar(gscale[:], tmp[:], 1.0 / (4 * 9) ** 2, None, ALU.mult))
                own = owner[:, :, None].to_broadcast([P, B, GROUPS])
                for src, dst in ((mean1, strip_mean), (gscale, strip_scale)):
                    then(V.tensor_tensor(tmp[:].rearrange("p (b g) -> p b g", b=B),
                                         src[:].rearrange("p (b g) -> p b g", b=B), own, ALU.mult))
                    then(V.tensor_reduce(dst[:], tmp[:].rearrange("p (b g) -> p g b", b=B), axis=AX.X, op=ALU.add))

            @block.scalar
            def _(act):
                A = nc.scalar
                act.wait_ge(roots_in, 1)
                A.activation(root[:], v0[:], ACT.Sqrt).then_inc(roots, 1)
                act.wait_ge(raw_in, 16 * 3)
                A.activation(eh_hi[:], eh_raw[:], ACT.Copy)
                A.activation(ew_hi[:], ew_raw[:], ACT.Copy).then_inc(tables_hi, 1)
                for v, (i, scale) in enumerate([(0, 1.0), (0, -1.0), (1, 1.0), (1, 2.0)]):
                    A.activation(hmat[:, :, v], hm_raw[:, :, i], ACT.Copy, scale=scale)

                def transposed(s):
                    act.wait_ge(xt_ps, s + 1)
                    xp = small[:].rearrange("p (b r q) -> p r q b", b=B, r=2)
                    for v, (r, scale) in enumerate([(0, 1.0), (1, -1.0), (1, 1.0), (0, 1.0)]):
                        last = A.activation(xt[:, :, :, v], xp[:, r], ACT.Copy, scale=scale)
                    last.then_inc(xt_done, 1)

                transposed(0)

                def part(s, last=False):
                    act.wait_ge(mixed, s + 1)
                    need(act, back, s * TB)
                    A.activation(os[:].rearrange("p v (k q) -> p k q v", k=4),
                                 ops[:, :, 0:256].rearrange("p k (q v) -> p k q v", v=32), ACT.Copy).then_inc(os_done, 1)
                    if not last:
                        transposed(s + 1)
                    need(act, mx_used, s)
                    flat = mx[:].rearrange("r b v a d -> r (b v a d)")
                    for i in range(TB):
                        act.wait_ge(back, s * TB + i + 1)
                        A.activation(flat[:, i * 512:(i + 1) * 512], ops_t[i % 2][:], ACT.Copy).then_inc(back_used, 1)
                    act.wait_ge(back_used, (s + 1) * TB)
                    alone(act, passed)
                    for v in range(2):
                        A.activation(of_part(split[0:RI, :, :, v], s), mx[:, :, v], ACT.Copy).then_inc(modes_hi, 1)

                parts(act, part)
                act.wait_ge(roots_in, 2)
                A.activation(root[:], v1[:], ACT.Sqrt).then_inc(roots, 1)

            @block.tensor
            def _(pe):
                T = nc.tensor
                agv = ag[:].rearrange("p b g s -> p (b g) s")
                T.matmul(small[:, 0:BG], ones[:], agv[:, :, 0], start=True, stop=True).then_inc(sums, 1)
                pe.wait_ge(sums_in, 1)
                T.matmul(small[:, 0:BG], ones[:], v1[:], start=True, stop=True).then_inc(sums, 1)
                pe.wait_ge(roots_in, 1)

                def transposes(s):
                    pe.wait_ge(sx_done, s + 1)
                    need(pe, xt_done, s)
                    alone(pe, passed)
                    for b in range(B):
                        last = T.transpose(small[:, b * RI:(b + 1) * RI],
                                           sx[:, b].rearrange("r a c -> r (a c)"), ident[0:RI, 0:RI])
                    last.then_inc(xt_ps, 1)

                transposes(0)

                def part(s, last=False):
                    pe.wait_ge(xt_done, s + 1)
                    pe.wait_ge(wst_done, s + 1)
                    need(pe, os_done, s)
                    alone(pe, passed)
                    for turn in range(4):
                        for q in range(MODES // 4):
                            for a in range(4):
                                k = (turn + a) % 4
                                rows = slice(C * a, C * (a + 1))
                                ins = T.matmul(
                                    ops[rows, k, q * 32:(q + 1) * 32], wst[rows, k * (MODES // 4) + q],
                                    xt[rows, k * (MODES // 4) + q].rearrange("c b v -> c (b v)"),
                                    start=True, stop=True)
                    ins.then_inc(mixed, 1)
                    if not last:
                        transposes(s + 1)
                    pe.wait_ge(os_done, s + 1)
                    for i in range(TB):
                        need(pe, back_used, s * TB + i - 1)
                        alone(pe, passed)
                        for k in range(4):
                            b, v = 2 * i + k // 2, k % 2
                            ins = T.transpose(
                                ops_t[i % 2][:, k * P:(k + 1) * P],
                                os[:, 4 * b + 2 * v:4 * b + 2 * v + 2].rearrange("p r q -> p (r q)"), ident[:])
                        ins.then_inc(back, 1)

                parts(pe, part)
                pe.wait_ge(sums_in, 2)
                T.matmul(small[:, 0:BG], ws_t[:, 0], sxy[:, 0], start=True, stop=False)
                T.matmul(small[:, 0:BG], ws_t[:, 1], sxy[:, 1], start=False, stop=True).then_inc(sums, 1)
                T.matmul(ops[:, 0, 0:BG], onerow[:], my[:], start=True, stop=True).then_inc(sums, 1)

            @block.sync
            def _(sp):
                for t, name in ((eh_raw, "eh"), (ew_raw, "ew"), (hm_raw, "hm")):
                    sp.dma_start(t[:], tab[name]).then_inc(raw_in, 16)
                sp.wait_ge(modes_lo, PARTS)
                for b in range(B):
                    sp.dma_start(od[b], split[:, b].rearrange("r d v p -> r (d v p)").bitcast(F32)).then_inc(stored, 16)
                sp.wait_ge(stored, 16 * B)
                sp.wait_ge(patched, 1)
                modes = od.rearrange("b r (c v p) -> r b c v p", v=2, c=C)
                for part in range(2):
                    sp.dma_start(modes[part * RI:part * RI + 1, :, :, 0, 0], dc_parts[:, part].bitcast(F32),
                                 allow_slow_non_contiguous=True).then_inc(stored, 16)
                sp.wait_ge(stored, 16 * (B + 2))


def gradient_pass(nc, sb, ps, sem, x, out, od, strip_y, ew_hi, ew_lo, eh_hi, eh_lo, hmat, mean1, gscale,
                  strip_mean, strip_scale, eps_t):
    LAG_LO, LAG_GRAD, LAG_SQ, LAG_SUM, LAG_MAG, LAG_OUT = 1, 2, 3, 3, 4, 4
    UNROLL = 4
    PER = GROUPS // UNROLL
    ROUNDS = BLOCKS * PER
    SLOTS = C // ROUNDS
    with ExitStack() as gr:
        xb = sb("xb", [P, 2, WB, C], at=gr)
        g_t = sb("g_t", [P, 2, C, WB], F32R, at=gr)
        stage = sb("stage", [P, SLOTS, 2, 2 * MODES], F32R, at=gr)
        x1 = sb("x1", [P, RING, GROUP, WB], at=gr)
        pr = sb("pr", [P, 2, GROUP, PAIRS + 1], at=gr)
        phi = sb("phi", [P, 2, GROUP, PAIRS + 1], F32R, at=gr)
        plo = sb("plo", [P, 2, GROUP, PAIRS + 1], F32R, at=gr)
        sq = sb("sq", [P, 2, 2, 512], at=gr)
        ssum = sb("ssum", [P, 2, 512], at=gr)
        mag = sb("mag", [P, 2, 512], at=gr)
        ghost = sb("ghost", [P, 4, C], at=gr)
        yps = ps("yps", [P, 2, 512], gr)
        gps = [ps(f"gps{i}", [P, 2, 512], gr) for i in range(2)]
        mps = ps("mps", [P, 512], gr)
        aside = sb("aside", [STRIP, SLOTS, WB], at=gr)

        x_in, ghosts = sem("x_in"), sem("ghosts")
        x_out = [sem(f"x_out{i}") for i in range(2)]
        ghost_link = sem("ghost_link")
        y_done, x1_done, pairs_done = sem("y_done"), sem("x1_done"), sem("pairs_done")
        hi_done, lo_done, grad_done = sem("hi_done"), sem("lo_done"), sem("grad_done")
        sq_done, sum_done, mag_done, out_done = sem("sq_done"), sem("sum_done"), sem("mag_done"), sem("out_done")
        staged = [sem(f"staged{i}") for i in range(SLOTS)]
        first_staged = sem("first_staged")
        g_ps, g_hi, g_lo = sem("g_ps"), sem("g_hi"), sem("g_lo")
        passed = sem("gradient_passed")
        strip_done, strip_copied = sem("strip_done"), sem("strip_copied")
        strip_out = [sem(f"strip_out{i}") for i in range(SLOTS)]
        strip_in = sem("strip_in")

        def steps(engine, n, emit, written_out=False):
            for k in range(2 if isinstance(n, int) and n == TURNS else BLOCKS):
                if (k == 0 and isinstance(n, int) and n == 0) or written_out:
                    for g in range(GROUPS):
                        emit(k, g // UNROLL * UNROLL, g % UNROLL)
                    continue
                for j in range(UNROLL):
                    emit(k, 0, j)
                with engine.Fori(1, GROUPS // UNROLL) as i:
                    for j in range(UNROLL):
                        emit(k, i * UNROLL, j)

        def turns(engine, turn):
            turn(0)
            with engine.Fori(1, TURNS - 1) as n:
                turn(n)
            turn(TURNS - 1)
            turn(TURNS)

        class Step:

            def __init__(self, n, k, g0, j, lag=0):
                self.number = n * STEPS + k * GROUPS + g0 + (j - lag)
                if isinstance(g0, int) and g0 + j < lag:
                    k, g0 = k - 1, g0 + GROUPS
                    if k < 0:
                        k, n = BLOCKS - 1, n - 1
                self.strip = isinstance(n, int) and n == TURNS
                self.exists = not (isinstance(n, int) and n < 0) and not (self.strip and k == 2)
                self.turn, self.block, self.slot = n, k, k % 2
                self.g = g0 + (j - lag)
                self.ring = (g0 + (j - lag + RING)) % RING
                self.two = (j - lag) % 2
                self.variant = 2 if self.strip else VARIANT[k]

            def of_group(self, table, strip_table):
                if self.strip:
                    return strip_table[:, bass.ds(self.g, 1)]
                return table[:, bass.ds(self.turn % B * GROUPS + self.g, 1)]

        last_steps = [(2, 0, j) for j in range(LAG_OUT)]

        def spreads(n, j=1):
            return j % 2 == 1 and not (isinstance(n, int) and n >= TURNS - 1)

        def asides(n, j=0):
            return j % 2 == 0 and not (isinstance(n, int) and n >= TURNS)

        first_modes = g_t[:, 1].rearrange("p c w -> p (c w)")[:, 0:C * P].rearrange("p (c t v) -> p c t v", c=C, t=2)
        banks = [mps[:, 0:WB], yps[:, 0, 0:WB], yps[:, 1, 0:WB], gps[0][:, 0, 0:WB]]

        with nc.Block() as block:
            @block.sync
            def _(sp):
                CUT = HALF // 2

                def load(n, k, part):
                    half = n // B
                    w0, size = (0, CUT) if part == 0 else (CUT, WIN - CUT)
                    src = x[n % B, ROW0[k]:ROW0[k] + P, bass.ds(half * (W - WIN) + w0, size), :]
                    sp.dma_start(xb[:, k % 2, bass.ds(half * -2 + 2 + w0, size), :], src).then_inc(x_in, 16)

                def load_strips(half):
                    w0, at = half * (W - WIN), 2 - 2 * half
                    for b in range(B):
                        sp.dma_start(xb[b * STRIP:(b + 1) * STRIP, half, at:at + WIN, :],
                                     x[b, STRIP0:, w0:w0 + WIN, :]).then_inc(x_in, 16)

                def load_strip_y(half):
                    sp.wait_ge(y_done, (TURNS - 1 + half) * STEPS)
                    sp.wait_ge(strip_done, (TURNS - 1 + half) * C)
                    for j in range(SLOTS):
                        sp.wait_ge(strip_out[j], 16 * (half + 1) * B * ROUNDS)
                    dst = g_t[:, half].rearrange("p c w -> p (c w)").bitcast(F32)
                    sp.dma_start(dst, strip_y[half].rearrange("b r c w -> (b r) (c w)")).then_inc(strip_in, 16)

                def store(n, k, part):
                    first, last = OUT[k]
                    cut = first + (last - first) // 16 * 16
                    for a, z in ((first, cut), (cut, last)):
                        r, w0 = a - ROW0[k], part * CUT
                        sp.dma_start(out[n % B, a:z, bass.ds((n // B) * HALF + w0, CUT), :],
                                     xb[r:r + z - a, k % 2, 2 + w0:2 + w0 + CUT, :]).then_inc(x_out[part], 16)

                def turn(n, last=False):
                    for k in range(BLOCKS):
                        sp.wait_ge(out_done, n * STEPS + (k + 1) * GROUPS)
                        for part in range(2):
                            store(n, k, part)
                        if last and k in (0, BLOCKS - 1):
                            if k > 0:
                                sp.wait_ge(strip_in, 16)
                            load_strip_y(1 if k else 0)
                        strips = last and k == BLOCKS - 1
                        sp.wait_ge(x_in, 2 * 16 * (n * BLOCKS + k + 2 - strips) + 16 * B * strips)
                        for part in range(2):
                            sp.wait_ge(x_out[part], 2 * 16 * (n * BLOCKS + k + 1))
                            if not (last and k >= 2):
                                load(n + (k + 2) // BLOCKS, (k + 2) % BLOCKS, part)
                        if last and k >= 2:
                            load_strips(k - 2)

                for twice in range(2):
                    sp.dma_start(first_modes[:, :, twice].bitcast(F32), od[0].rearrange("r (c v) -> r c v", c=C)
                                 ).then_inc(first_staged, 16)
                for part in range(2):
                    load(0, 0, part)
                sp.wait_ge(x_in, 2 * 16)
                for part in range(2):
                    load(0, 1, part)
                with sp.Fori(0, TURNS - 1) as n:
                    turn(n)
                turn(TURNS - 1, last=True)
                for half in range(2):
                    sp.wait_ge(out_done, TURNS * STEPS + (half + 1) * GROUPS)
                    for b in range(B):
                        r = b * STRIP + OUT[-1][1] - STRIP0
                        sp.dma_start(out[b, OUT[-1][1]:, half * HALF:(half + 1) * HALF, :],
                                     xb[r:(b + 1) * STRIP, half, 2:2 + HALF, :]).then_inc(x_out[half], 16)
                for part in range(2):
                    sp.wait_ge(x_out[part], 2 * 16 * TURNS * BLOCKS + 16 * B)

            @block.gpsimd
            def _(pool):
                G = nc.gpsimd
                def ghosts_of(n, k):
                    slot, half, unit = k % 2, (k if isinstance(n, int) and n == TURNS else n // B), n * BLOCKS + k
                    loads = 2 * 16 * (unit + 1)
                    if isinstance(n, int) and n == TURNS:
                        loads = 2 * 16 * TURNS * BLOCKS + 16 * (k + 1) * B
                    pool.wait_ge(x_in, loads)

                    def col(left, right):
                        return xb[:, slot, bass.ds(half * (right - left) + left, 1), :].rearrange("p w c -> p (w c)")
                    edge, inner = col(2, WIN - 1), col(3, WIN - 2)
                    near, far = col(1, WIN), col(0, WIN + 1)

                    def then(step, ins):
                        ins.then_inc(ghost_link, 1)
                        pool.wait_ge(ghost_link, 4 * unit + step + 1)
                        alone(pool, passed)

                    alone(pool, passed)
                    then(0, G.tensor_tensor(ghost[:, 0], edge, inner, ALU.add))
                    then(1, G.tensor_scalar(ghost[:, 1], ghost[:, 0], 0.5, None, ALU.mult))
                    G.tensor_copy(near, ghost[:, 1])
                    then(2, G.tensor_tensor(ghost[:, 2], edge, ghost[:, 1], ALU.add))
                    then(3, G.tensor_scalar(ghost[:, 3], ghost[:, 2], -1.0, None, ALU.mult))
                    G.tensor_copy(far, ghost[:, 3]).then_inc(ghosts, 1)

                def fetch(m, i, slot):
                    src = od[m % B].rearrange("r (d v) -> r d v", d=C)[:, bass.ds(i * SLOTS + slot, 1), :]
                    pool.dma_start(stage[:, slot].bitcast(F32), src.to_broadcast([P, 2, 2 * MODES])).then_inc(staged[slot], 16)

                for slot in range(SLOTS):
                    fetch(1, 0, slot)
                ghosts_of(0, 0)

                def put_aside(n, i, slot):
                    pool.wait_ge(strip_copied, n * C + SLOTS * i + slot + 1)
                    dst = strip_y[n // B, n % B, :, bass.ds(i * SLOTS + slot, 1), :].rearrange("r c w -> r (c w)")
                    pool.dma_start(dst, aside[:, slot]).then_inc(strip_out[slot], 16)

                def fetch_next(n, i, slot):
                    if not spreads(n):
                        return
                    pool.wait_ge(g_ps, (n + 1) * C + SLOTS * i + slot + 1)
                    alone(pool, passed)
                    following = n * ROUNDS + i + 1
                    fetch(following // ROUNDS + 1, following % ROUNDS, slot)

                def turn(n):
                    if isinstance(n, int) and n == TURNS:
                        ghosts_of(TURNS, 1)
                        return
                    for k in range(BLOCKS):
                        with pool.Fori(k * PER, (k + 1) * PER - 1) as i:
                            for slot in range(SLOTS):
                                put_aside(n, i, slot)
                                fetch_next(n, i, slot)
                        for slot in range(SLOTS):
                            put_aside(n, (k + 1) * PER - 1, slot)
                            fetch_next(n, (k + 1) * PER - 1, slot)
                            if slot == 0:
                                ghosts_of(n + (k + 1) // BLOCKS, (k + 1) % BLOCKS)

                turns(pool, turn)
                for slot in range(SLOTS):
                    pool.wait_ge(staged[slot], 16 * ((TURNS - 1) * ROUNDS + 1))

            @block.tensor
            def _(pe):
                T = nc.tensor

                def make_g(m, dst, modes):
                    half = [t[:, bass.ds(m // B % 2, 1), :].rearrange("r h w -> r (h w)") for t in (ew_lo, ew_hi)]
                    T.matmul(dst, modes, half[0], start=True, stop=False)
                    T.matmul(dst, modes, half[1], start=False, stop=True).then_inc(g_ps, 1)

                def spread(n, i, slot):
                    pe.wait_ge(staged[slot], 16 * (n * ROUNDS + i + 1))
                    pe.wait_ge(g_lo, (n + 1) * C + SLOTS * i + slot)
                    pe.wait_ge(strip_copied, n * C + SLOTS * i + slot + 1)
                    alone(pe, passed)
                    make_g(n + 1, mps[:, 0:WB], stage[:, slot].rearrange("r t v -> r (t v)"))

                def inverse_h(dst, s_turn, c, cols):
                    rhs = g_t[:, s_turn % 2, bass.ds(c, 1), :].rearrange("p c w -> p (c w)")
                    T.matmul(dst, eh_lo[:, cols], rhs, start=True, stop=False)
                    return T.matmul(dst, eh_hi[:, cols], rhs, start=False, stop=True)

                def put_aside(n, i, slot):
                    need(pe, strip_copied, n * C + SLOTS * i + slot)
                    pe.wait_ge(g_lo, (n + 1) * C + (SLOTS * i + slot if spreads(n) else 0))
                    alone(pe, passed)
                    cols = slice(BLOCKS * P, BLOCKS * P + STRIP)
                    inverse_h(mps[0:STRIP, 0:WB], n, i * SLOTS + slot, cols).then_inc(strip_done, 1)

                def y(s):
                    need(pe, x1_done, s.number)
                    alone(pe, passed)
                    for ch in range(GROUP):
                        last = inverse_h(yps[:, ch, 0:WB], s.turn, s.g * GROUP + ch,
                                         slice(s.block * P, (s.block + 1) * P))
                    last.then_inc(y_done, 1)

                def grad(s):
                    if not s.exists:
                        return
                    pe.wait_ge(lo_done, s.number + 1)
                    need(pe, sq_done, s.number - 1)
                    taps = [[(0, 0), (1, 3)], [(2, 0), (3, 1), (3, 2), (2, 3)]]
                    for d in range(2):
                        todo = [(m, w, part) for m, w in taps[d] for part in (plo, phi)]
                        for i, (m, w, part) in enumerate(todo):
                            last = T.matmul(gps[s.two][:, d], hmat[:, s.variant, m],
                                            part[:, s.two, :, w:w + HALF],
                                            start=(i == 0), stop=(i == len(todo) - 1))
                    last.then_inc(grad_done, 1)

                pe.wait_ge(first_staged, 2 * 16)
                for c in range(C):
                    need(pe, g_lo, c - UNROLL + 1)
                    make_g(0, banks[c % UNROLL], first_modes[:, c].rearrange("r t v -> r (t v)"))

                def turn(n):
                    def emit(k, g0, j):
                        s = Step(n, k, g0, j)
                        if not s.strip:
                            if k == 0:
                                first = isinstance(n, int) and n == 0
                                pe.wait_ge(g_lo, C if first else n * C + GROUP * (g0 + j + 1))
                            y(s)
                        grad(Step(n, k, g0, j, LAG_GRAD))
                        i = k * PER + g0 // UNROLL
                        if spreads(n, j):
                            spread(n, i, j // 2)
                        if asides(n, j):
                            put_aside(n, i, j // 2)
                    steps(pe, n, emit)

                turns(pe, turn)
                for k, g0, j in last_steps[:LAG_GRAD]:
                    grad(Step(TURNS, k, g0, j, LAG_GRAD))

            @block.scalar
            def _(act):
                A = nc.scalar

                def high(m, c, src):
                    act.wait_ge(g_ps, m * C + c + 1)
                    alone(act, passed)
                    dst = g_t[:, m % 2, bass.ds(c, 1), :].rearrange("p c w -> p (c w)")
                    A.activation(dst, src, ACT.Copy).then_inc(g_hi, 1)

                def put_aside(n, i, slot):
                    act.wait_ge(strip_done, n * C + SLOTS * i + slot + 1)
                    need(act, strip_out[slot], 16 * (n * ROUNDS + i))
                    A.activation(aside[:, slot], mps[0:STRIP, 0:WB], ACT.Copy).then_inc(strip_copied, 1)

                def magnitude(s):
                    if not s.exists:
                        return
                    act.wait_ge(sum_done, s.number + 1)
                    need(act, out_done, s.number - 1)
                    alone(act, passed)
                    scale = s.of_group(gscale, strip_scale)
                    A.activation(mag[:, s.two], ssum[:, s.two], ACT.Sqrt, bias=eps_t[:], scale=scale).then_inc(mag_done, 1)

                def squares(s):
                    if not s.exists:
                        return
                    act.wait_ge(grad_done, s.number + 1)
                    need(act, sum_done, s.number - 1)
                    A.activation(sq[:, s.two], gps[s.two][:], ACT.Square).then_inc(sq_done, 1)

                def high_pairs(s):
                    act.wait_ge(pairs_done, s.number + 1)
                    need(act, grad_done, s.number - 1)
                    A.activation(phi[:, s.two, :, 0:PAIRS], pr[:, s.two, :, 0:PAIRS], ACT.Copy).then_inc(hi_done, 1)

                with act.Fori(0, C // UNROLL) as i:
                    for j in range(UNROLL):
                        high(0, i * UNROLL + j, banks[j])

                def turn(n):
                    def emit(k, g0, j):
                        magnitude(Step(n, k, g0, j, LAG_MAG))
                        squares(Step(n, k, g0, j, LAG_SQ))
                        high_pairs(Step(n, k, g0, j))
                        i = k * PER + g0 // UNROLL
                        if spreads(n, j):
                            high(n + 1, SLOTS * i + j // 2, mps[:, 0:WB])
                        if asides(n, j):
                            put_aside(n, i, j // 2)
                    steps(act, n, emit)

                turns(act, turn)
                for k, g0, j in last_steps:
                    magnitude(Step(TURNS, k, g0, j, LAG_MAG))
                    if j < LAG_SQ:
                        squares(Step(TURNS, k, g0, j, LAG_SQ))

            @block.vector
            def _(dve):
                V = nc.vector

                def low(m, c, src):
                    dve.wait_ge(g_hi, m * C + c + 1)
                    dst = g_t[RI:P, m % 2, bass.ds(c, 1), :].rearrange("p c w -> p (c w)")
                    V.tensor_tensor(dst, src[RI:P], dst.bitcast(F32), ALU.subtract).then_inc(g_lo, 1)

                def add_y(s):
                    if s.strip:
                        y = g_t[:, s.block, bass.ds(s.g * GROUP, GROUP)].bitcast(F32)
                    else:
                        dve.wait_ge(y_done, s.number + 1)
                        y = yps[:, :, 0:WB]
                    src = xb[:, s.slot, :, bass.ds(s.g * GROUP, GROUP)].rearrange("p w c -> p c w")
                    V.tensor_tensor(x1[:, s.ring], src, y, ALU.add).then_inc(x1_done, 1)

                def low_pairs(s):
                    if not s.exists:
                        return
                    dve.wait_ge(hi_done, s.number + 1)
                    need(dve, grad_done, s.number - 1)
                    V.tensor_tensor(plo[:, s.two, :, 0:PAIRS], pr[:, s.two, :, 0:PAIRS],
                                    phi[:, s.two, :, 0:PAIRS].bitcast(F32), ALU.subtract).then_inc(lo_done, 1)

                def pairs(s):
                    dve.wait_ge(x1_done, s.number + 1)
                    V.tensor_tensor(pr[:, s.two, :, 0:PAIRS], x1[:, s.ring, :, 0:PAIRS],
                                    x1[:, s.ring, :, 1:WB], ALU.add).then_inc(pairs_done, 1)

                def add_squares(s):
                    if not s.exists:
                        return
                    dve.wait_ge(sq_done, s.number + 1)
                    need(dve, mag_done, s.number - 1)
                    V.tensor_tensor(ssum[:, s.two], sq[:, s.two, 0], sq[:, s.two, 1], ALU.add).then_inc(sum_done, 1)

                def result(s):
                    if not s.exists:
                        return
                    dve.wait_ge(mag_done, s.number + 1)
                    dst = xb[:, s.slot, 2:2 + HALF, bass.ds(s.g * GROUP, GROUP)].rearrange("p w c -> p c w")
                    V.scalar_tensor_tensor(dst, x1[:, s.ring, :, 2:2 + HALF],
                                           s.of_group(mean1, strip_mean),
                                           mag[:, s.two].rearrange("p (c w) -> p c w", c=GROUP),
                                           ALU.add, ALU.add).then_inc(out_done, 1)

                with dve.Fori(0, C // UNROLL) as i:
                    for j in range(UNROLL):
                        low(0, i * UNROLL + j, banks[j])

                def turn(n):
                    def emit(k, g0, j):
                        if isinstance(g0, int) and g0 + j == 0:
                            dve.wait_ge(ghosts, n * BLOCKS + k + 1)
                            if isinstance(n, int) and n == TURNS:
                                dve.wait_ge(strip_in, 16 * (k + 1))
                        add_y(Step(n, k, g0, j))
                        low_pairs(Step(n, k, g0, j, LAG_LO))
                        pairs(Step(n, k, g0, j))
                        add_squares(Step(n, k, g0, j, LAG_SUM))
                        result(Step(n, k, g0, j, LAG_OUT))
                        if spreads(n, j):
                            low(n + 1, SLOTS * (k * PER + g0 // UNROLL) + j // 2, mps[:, 0:WB])
                    steps(dve, n, emit, written_out=True)

                turns(dve, turn)
                for k, g0, j in last_steps:
                    if j < LAG_LO:
                        low_pairs(Step(TURNS, k, g0, j, LAG_LO))
                    if j < LAG_SUM:
                        add_squares(Step(TURNS, k, g0, j, LAG_SUM))
                    result(Step(TURNS, k, g0, j, LAG_OUT))


def kernel(x, L0_conv_W):
    import concourse.bacc as bacc
    from concourse.bass_utils import run_bass_kernel_spmd

    nc = bacc.Bacc("TRN2", target_bir_lowering=False, num_devices=1)
    tab = tables()
    arrays = {"x_dram": np.ascontiguousarray(x), "w_dram": np.ascontiguousarray(L0_conv_W)}
    arrays.update({f"{n}_dram": a for n, a in tab.items()})
    aps = {n: nc.dram_tensor(n, a.shape, mybir.dt.from_np(a.dtype), kind="ExternalInput").ap()
           for n, a in arrays.items()}
    out = nc.dram_tensor("out_dram", (B, H, W, C), F32, kind="ExternalOutput").ap()
    od = nc.dram_tensor("mixed_modes", (B, P, 2 * C * MODES), F32, kind="Internal").ap()
    strip_y = nc.dram_tensor("strip_y", (2, B, STRIP, C, WB), F32, kind="Internal").ap()
    spectral_gradient_kernel(nc, aps["x_dram"], aps["w_dram"], {n: aps[f"{n}_dram"] for n in tab}, out, od, strip_y)
    r = run_bass_kernel_spmd(nc, [arrays], core_ids=[0])
    return r.results[0]["out_dram"]
```
